# Optimizing a Trainium2 kernel written in Bass

```python
import numpy as np
import jax
import jax.numpy as jnp

def _softmax(x, axis=-1):
    return jax.nn.softmax(x, axis=axis)

def _gelu(x):
    return jax.nn.gelu(x, approximate=True)

def _silu(x):
    return jax.nn.silu(x)

def _sigmoid(x):
    return jax.nn.sigmoid(x)

def _layernorm(x, axis=-1, eps=1e-05):
    m = jnp.mean(x, axis=axis, keepdims=True)
    v = jnp.var(x, axis=axis, keepdims=True)
    return (x - m) / jnp.sqrt(v + eps)

def _scatter_add(tgt, idx, src, axis=0):
    return tgt.at[idx].add(src)

def _segment_sum(src, seg, n):
    return jax.ops.segment_sum(src, seg, n)
kernel_name = 'mk_xattn_ffn_d1_seqx_r8_465f9f'

def setup_inputs(seed: int=0):
    np.random.seed(seed)
    _w = jnp.asarray

    def _rec_inputs():
        import jax
        import jax.numpy as jnp
        _rk = jax.random.key(seed)
        x = -0.0003929 + 0.9999 * jax.random.normal(jax.random.fold_in(_rk, 1), (32, 64, 512), jnp.float32)
        _lenS = 64 - jax.random.randint(jax.random.fold_in(_rk, 7), (32,), 0, max(1, 64 // 4) + 1, jnp.int32)
        _lenS2 = 64 - jax.random.randint(jax.random.fold_in(_rk, 8), (32,), 0, max(1, 64 // 4) + 1, jnp.int32)
        _ctx_4096P = jax.random.normal(jax.random.fold_in(_rk, 11), (32, 16, 512), jnp.float32)
        _ctx_4096c = jax.random.dirichlet(jax.random.fold_in(_rk, 511), 0.3 * jnp.ones((16,), jnp.float32), (32, 64))
        _ctx_4096t = jnp.einsum('bsk,bkd->bsd', _ctx_4096c, _ctx_4096P)
        _ctx_4096t = _ctx_4096t * jax.lax.rsqrt(jnp.mean(jnp.square(_ctx_4096t)) + 1e-12) * 0.953939
        ctx_4096 = 2.81802e-05 + 1.00001 * (_ctx_4096t + 0.3 * jax.random.normal(jax.random.fold_in(_rk, 611), (32, 64, 512), jnp.float32))
        return (x, ctx_4096)
    x, ctx_4096 = _rec_inputs()

    def _L0_xattn_setup():
        import jax, jax.numpy as jnp
        import numpy as np
        HID = 512
        NHEAD = 32
        NKV = 8
        HDIM = 128
        G = NHEAD // NKV
        key = jax.random.key(seed)
        ks = jax.random.split(key, 6)
        s = 0.02
        B, L = (2, 256)
        return {'query': jax.random.normal(ks[0], (B, L, HID), jnp.float32), 'kv': jax.random.normal(ks[1], (B, L, HID), jnp.float32), 'Wq': jax.random.normal(ks[2], (HID, NHEAD * HDIM), jnp.float32) * s, 'bq': jnp.zeros((NHEAD * HDIM,), jnp.float32), 'Wkv': jax.random.normal(ks[3], (HID, 2 * NKV * HDIM), jnp.float32) * s, 'bkv': jnp.zeros((2 * NKV * HDIM,), jnp.float32), 'Wo': jax.random.normal(ks[4], (NHEAD * HDIM, HID), jnp.float32) * s, 'bo': jnp.zeros((HID,), jnp.float32)}
    _L0_xattn_all = _L0_xattn_setup()
    _L0_xattn_in = {k: v for k, v in _L0_xattn_all.items() if k in ('Wq', 'bq', 'Wkv', 'bkv', 'Wo', 'bo')}
    del _L0_xattn_all

    def _L0_ffn_setup():
        import jax, jax.numpy as jnp
        import numpy as np
        B_, S, D = (4, 512, 512)
        E, R, O = (8, 16, 512)
        TOP_K = 2
        SCALING = 8.0 / R
        key = jax.random.key(seed)
        ks = jax.random.split(key, 5)
        x = jax.random.normal(ks[0], (B_, S, D), dtype=jnp.float32)
        router_w = jax.random.normal(ks[1], (E, D), dtype=jnp.float32) * (1.0 / np.sqrt(D))
        router_b = jax.random.normal(ks[2], (E,), dtype=jnp.float32) * 0.01
        A = jax.random.normal(ks[3], (E, R, D), dtype=jnp.float32) * (1.0 / np.sqrt(D))
        Bm = jax.random.normal(ks[4], (E, O, R), dtype=jnp.float32) * 0.02
        return {'x': x, 'router_w': router_w, 'router_b': router_b, 'A': A, 'Bm': Bm}
    _L0_ffn_all = _L0_ffn_setup()
    _L0_ffn_in = {k: v for k, v in _L0_ffn_all.items() if k in ('router_w', 'router_b', 'A', 'Bm')}
    del _L0_ffn_all
    return {'x': x, 'ctx_4096': ctx_4096, 'L0_xattn_Wq': _L0_xattn_in['Wq'], 'L0_xattn_bq': _L0_xattn_in['bq'], 'L0_xattn_Wkv': _L0_xattn_in['Wkv'], 'L0_xattn_bkv': _L0_xattn_in['bkv'], 'L0_xattn_Wo': _L0_xattn_in['Wo'], 'L0_xattn_bo': _L0_xattn_in['bo'], 'L0_ffn_router_w': _L0_ffn_in['router_w'], 'L0_ffn_router_b': _L0_ffn_in['router_b'], 'L0_ffn_A': _L0_ffn_in['A'], 'L0_ffn_Bm': _L0_ffn_in['Bm']}

def reference(x, ctx_4096, L0_xattn_Wq, L0_xattn_bq, L0_xattn_Wkv, L0_xattn_bkv, L0_xattn_Wo, L0_xattn_bo, L0_ffn_router_w, L0_ffn_router_b, L0_ffn_A, L0_ffn_Bm):
    import jax
    import jax.numpy as jnp

    def _L0_xattn_ref(query, kv, Wq, bq, Wkv, bkv, Wo, bo):
        import jax, jax.numpy as jnp
        import numpy as np
        HID = 512
        NHEAD = 32
        NKV = 8
        HDIM = 128
        G = NHEAD // NKV
        B, L, _ = query.shape
        Lk = kv.shape[1]
        scale = jnp.asarray(1.0 / np.sqrt(HDIM), query.dtype)
        q = (query @ Wq + bq).reshape(B, L, NKV, G, HDIM)
        k_, v_ = jnp.split(kv @ Wkv + bkv, 2, axis=-1)
        k = k_.reshape(B, Lk, NKV, HDIM)
        v = v_.reshape(B, Lk, NKV, HDIM)
        scores = jnp.einsum('blkgd,bmkd->bkglm', q, k) * scale
        attn = jax.nn.softmax(scores, axis=-1)
        o = jnp.einsum('bkglm,bmkd->blkgd', attn, v).reshape(B, L, NHEAD * HDIM)
        return o @ Wo + bo

    def _L0_ffn_ref(x, router_w, router_b, A, Bm):
        import jax, jax.numpy as jnp
        import numpy as np
        B_, S, D = (4, 512, 512)
        E, R, O = (8, 16, 512)
        TOP_K = 2
        SCALING = 8.0 / R
        flat = x.reshape(-1, x.shape[-1])
        N = flat.shape[0]
        logits = flat @ router_w.T + router_b
        probs = jax.nn.softmax(logits, axis=-1)
        topv, topi = jax.lax.top_k(probs, TOP_K)
        gates = topv / jnp.sum(topv, axis=-1, keepdims=True)
        w = jnp.zeros((N, E), dtype=flat.dtype).at[jnp.arange(N)[:, None], topi].add(gates)
        h = jnp.einsum('nd,erd->ner', flat, A)
        hw = h * w[:, :, None]
        out = jnp.einsum('ner,eor->no', hw, Bm) * SCALING
        return out.reshape(*x.shape[:-1], O)
    x = x + _L0_xattn_ref(_layernorm(x, axis=-1), ctx_4096, L0_xattn_Wq, L0_xattn_bq, L0_xattn_Wkv, L0_xattn_bkv, L0_xattn_Wo, L0_xattn_bo)
    x = x + _L0_ffn_ref(_layernorm(x, axis=-1), L0_ffn_router_w, L0_ffn_router_b, L0_ffn_A, L0_ffn_Bm)
    return x

_drawn_inputs = setup_inputs


def setup_inputs(seed=0):
    import zlib

    import numpy as np

    out = dict(_drawn_inputs(seed))
    spreads = {'L0_xattn_bq': (0.0, 0.8), 'L0_xattn_bkv': (0.0, 0.1), 'L0_xattn_bo': (0.0, 0.1)}
    factors = {'L0_ffn_router_b': 8.0}
    for name, (base, spread) in spreads.items():
        noise = np.random.default_rng([zlib.crc32(name.encode()), seed]).standard_normal(out[name].shape)
        drawn = base * np.exp(spread * noise) if base else spread * noise
        out[name] = jnp.asarray(drawn.astype(out[name].dtype))
    for name, factor in factors.items():
        out[name] = (out[name] * factor).astype(out[name].dtype)
    return out
```

```python
from contextlib import ExitStack
from itertools import count

import concourse.bass as bass
import concourse.mybir as mybir

F32 = mybir.dt.float32
F32R = mybir.dt.float32r
ACT = mybir.ActivationFunctionType
ALU = mybir.AluOpType
AX = mybir.AxisListType.X

P = 128
B, L, D = 32, 64, 512
NH, NKV, HD = 32, 8, 128
G = NH // NKV
KC = D // P
TOK = B * L
HALVES = 2
HTOK = TOK // HALVES
TILES = HTOK // P
UTOK = 512
UNITS = HTOK // UTOK
UB = UTOK // L
UT = UTOK // P
HP = G // 2
E, R = 8, 16
ER = E * R
FN = ER + E
ATT_SCALE = 1.0 / float(HD) ** 0.5
LN_EPS = 1e-5
LORA_SCALE = 8.0 / R
SKIP = -3.0e38

PRO = 4
UNIT_TASKS = 2 + G + UT
HALF_TASKS = 2 * TILES + NKV * UNITS * UNIT_TASKS + 2 * TILES
QKV = G * HD + 2 * HD
ROUTER_STEPS = 1 + 5 + 1 + 5 + 6


def build(nc, x, ctx_in, wq, bq, wkv, bkv, wo, bo, router_w, router_b, A, Bm, out):
    ctx = ExitStack()
    with ctx:
        def sb(name, shape, dt=F32):
            return ctx.enter_context(nc.sbuf_tensor(name, shape, dt))

        def sem(name):
            return ctx.enter_context(nc.semaphore(name))

        x_rows = x.rearrange("b l d -> (b l) d")
        c_rows = ctx_in.rearrange("b l d -> (b l) d")
        out_rows = out.rearrange("b l d -> (b l) d")
        wq_v = wq.rearrange("(c p) n -> p c n", p=P)
        wkv_v = wkv.rearrange("(c p) n -> p c n", p=P)
        wo_v = wo.rearrange("(h p) n -> p h n", p=P)

        ident = sb("ident", [P, P])
        bias = sb("bias", [P, NKV, G + 2])
        g_bias = sb("g_bias", [P, G + 2])
        bo_bc = sb("bo_bc", [P, D])
        rb_bc = sb("rb_bc", [P, E])
        rev = sb("rev", [P, E])
        fw_h, fw_l = sb("fw_h", [P, KC, FN], F32R), sb("fw_l", [P, KC, FN], F32R)
        bm_h, bm_l = sb("bm_h", [P, D], F32R), sb("bm_l", [P, D], F32R)
        y = sb("y", [P, TILES, D])
        xT_h, xT_l = sb("xT_h", [P, KC, HTOK], F32R), sb("xT_l", [P, KC, HTOK], F32R)
        cT_h, cT_l = sb("cT_h", [P, KC, HTOK], F32R), sb("cT_l", [P, KC, HTOK], F32R)
        w_h, w_l = sb("w_h", [P, KC, QKV], F32R), sb("w_l", [P, KC, QKV], F32R)
        wo_h, wo_l = sb("wo_h", [P, G, D], F32R), sb("wo_l", [P, G, D], F32R)
        raw = sb("raw", [P, KC, QKV])
        raw_o = raw.rearrange("p c n -> p (c n)")[:, 0:G * D].rearrange("p (h n) -> p h n", h=G)
        qT_h, qT_l = sb("qT_h", [P, UB, G, L], F32R), sb("qT_l", [P, UB, G, L], F32R)
        fT_h, fT_l = (q.rearrange("p b h l -> p (b h l)").rearrange("p (c n) -> p c n", c=KC) for q in (qT_h, qT_l))
        kT = sb("kT", [P, UB, 2, L], F32R)
        work = sb("work", [P, 4 * D])
        s = work[:, 0:UB * HP * L].rearrange("p (n l) -> p n l", l=L)
        vT = work[:, 2 * D:4 * D].rearrange("p (b k l) -> p b k l", k=2, l=L)
        c_stage = work.rearrange("p (t d) -> p t d", d=D)
        bias_rows = work[0:NH + 2 * NKV, 2 * D:2 * D + HD]
        v_h, v_l = sb("v_h", [P, UB, HD], F32R), sb("v_l", [P, UB, HD], F32R)
        low_or_x = sb("low_or_x", [P, 2 * D])
        s_lo = low_or_x.rearrange("p (n l) -> p n l", l=L)
        xn = low_or_x.rearrange("p (t d) -> p t d", d=D)
        row_max = sb("row_max", [P, UB * HP])
        row_sum = sb("row_sum", [P, UB * HP])
        row_inv = sb("row_inv", [P, UB * HP])
        pT = sb("pT", [P, UB, HP, P], F32R)
        oT_h, oT_l = sb("oT_h", [P, G, UTOK], F32R), sb("oT_l", [P, G, UTOK], F32R)
        stats = sb("stats", [P, TILES, 6])
        mean, apart = sb("mean", [P, TILES]), sb("apart", [P, 4])
        rstd = sb("rstd", [P, TILES])
        exponent = sb("exponent", [P, 4])
        lg, lg2, sel1, sel2, mark = (
            work[:, 2 * D + i * TILES * E:2 * D + (i + 1) * TILES * E].rearrange("p (t e) -> p t e", e=E)
            for i in range(5))
        m1, m2, top, diff, gate1, gate2 = (
            work[:, 3 * D + i * TILES:3 * D + (i + 1) * TILES] for i in range(6))
        hw = work[:, 0:TILES * ER].rearrange("p (t n) -> p t n", n=ER)
        hwT_h, hwT_l = (o.rearrange("p h n -> p (h n)")[:, 0:TILES * P] for o in (oT_h, oT_l))

        ring = ctx.enter_context(nc.psum_tensor("ring", [P, 2, 512], F32))
        att = ctx.enter_context(nc.psum_tensor("att", [P, 4, 512], F32))
        turn = ctx.enter_context(nc.psum_tensor("turn", [P, 2, 512], F32))
        att_s = att.rearrange("p n (b k l) -> p (n b) k l", k=2, l=L)
        att_o = att.rearrange("p n (b h l) -> p n b h l", b=2, h=G)
        att_f = att.rearrange("p n (t f) -> p (n t) f", t=2)

        consts_loaded, ident_cleared, ident_ready = sem("consts_loaded"), sem("ident_cleared"), sem("ident_ready")
        w_loaded, wo_loaded = sem("w_loaded"), sem("wo_loaded")
        x_loaded = [sem(f"x_loaded{t}") for t in range(TILES)]
        c_loaded = [sem(f"c_loaded{t}") for t in range(4)]
        out_stored = [sem(f"out_stored{t}") for t in range(TILES)]
        half_stored = sem("half_stored")
        ring_filled, scores_filled = sem("ring_filled"), sem("scores_filled")
        v_turned, p_turned, o_filled = sem("v_turned"), sem("p_turned"), sem("o_filled")
        experts_filled, hw_turned = sem("experts_filled"), sem("hw_turned")
        pro_high, x_high, qk_high = sem("pro_high"), sem("x_high"), sem("qk_high")
        s_lo_copied, exp_done = sem("s_lo_copied"), sem("exp_done")
        v_high, p_high, o_high = sem("v_high"), sem("p_high"), sem("o_high")
        w_high, wo_high = sem("w_high"), sem("wo_high")
        gate_exp, hw_high = sem("gate_exp"), sem("hw_high")
        ring_emptied, s_added, max_done = sem("ring_emptied"), sem("s_added"), sem("max_done")
        sum_done, inv_done = sem("sum_done"), sem("inv_done")
        v_low, p_low, o_low, hw_low = sem("v_low"), sem("p_low"), sem("o_low"), sem("hw_low")
        ln_step, xn_ready, router_step, hw_ready = sem("ln_step"), sem("xn_ready"), sem("router_step"), sem("hw_ready")
        bias_ready = sem("bias_ready")
        gate_diff, var_ready = sem("gate_diff"), sem("var_ready")
        shifted, probs_ready, w_low, wo_low, resid_ready, rstd_ready = (
            sem("shifted"), sem("probs_ready"), sem("w_low"), sem("wo_low"), sem("resid_ready"), sem("rstd_ready"))

        FREE = 1
        N_CONSTS = 10

        def k_task(base, u, first):
            return base + 2 * TILES if first else base + 2 * TILES + UNIT_TASKS * u - UT

        def q_task(base, u, first, h):
            return k_task(base, u, first) + 1 + h

        def v_task(base, u, first):
            return k_task(base, u, first) + 1 + G

        def out_task(base, u, i):
            if isinstance(u, int) and u == NKV * UNITS:
                return ffn_task(base, i - UT)
            return base + 2 * TILES + UNIT_TASKS * u - UT + 2 + G + i

        def ffn_task(base, k):
            return base + 2 * TILES + NKV * UNITS * UNIT_TASKS + k

        block = ctx.enter_context(nc.Block())

        @block.sync
        def _(sp):
            def load_qkv(g):
                for dst, src, col in ((raw[:, :, 0:G * HD], wq_v, g * (G * HD)),
                                      (raw[:, :, G * HD:G * HD + HD], wkv_v, g * HD),
                                      (raw[:, :, G * HD + HD:QKV], wkv_v, g * HD + NKV * HD)):
                    sp.dma_start(dst, src[:, :, bass.ds(col, dst.shape[2])]).then_inc(w_loaded, 16)

            sp.dma_start(bias_rows[0:NH, :], bq.rearrange("(h p) -> h p", p=HD)).then_inc(consts_loaded, 16)
            sp.dma_start(bias_rows[NH:NH + 2 * NKV, :], bkv.rearrange("(h p) -> h p", p=HD)).then_inc(consts_loaded, 16)
            load_qkv(0)
            sp.dma_start(xn[:, 0, :], A.rearrange("e r d -> (e r) d")).then_inc(consts_loaded, 16)
            for c in range(KC):
                sp.dma_start(c_stage[:, 0, :].rearrange("p (c e r) -> p c e r", c=KC, e=E)[:, c],
                             Bm[:, c * P:(c + 1) * P, :].rearrange("e p r -> p e r")).then_inc(consts_loaded, 16)
            sp.dma_start(xn[0:E, 1, :], router_w).then_inc(consts_loaded, 16)
            sp.dma_start(bo_bc[:], bo.rearrange("(a d) -> a d", a=1).broadcast_to([P, D])).then_inc(consts_loaded, 16)
            sp.dma_start(rb_bc[:], router_b.rearrange("(a d) -> a d", a=1).broadcast_to([P, E])).then_inc(consts_loaded, 16)
            sp.wait_ge(ring_filled, PRO)
            with sp.Fori(0, HALVES) as half:
                base = half * HALF_TASKS + PRO

                def load_c(t):
                    sp.dma_start(c_stage[:, t % 4, :],
                                 c_rows[bass.ds(half * HTOK + t * P, P), :]).then_inc(c_loaded[t % 4], 16)

                def load_x(t):
                    sp.dma_start(y[:, t, :], x_rows[bass.ds(half * HTOK + t * P, P), :]).then_inc(x_loaded[t], 16)

                sp.wait_ge(hw_turned, half * 2 + FREE)
                for t in range(4):
                    load_c(t)
                for t in range(4):
                    load_x(t)
                for t in range(4, TILES):
                    sp.wait_ge(ring_filled, base + t - 4 + 1)
                    load_c(t)
                for t in range(4, TILES):
                    load_x(t)
                with sp.Fori(0, NKV) as g:
                    step = half * NKV + g
                    sp.wait_ge(w_low, step * KC + KC)
                    sp.dma_start(raw_o, wo_v[:, bass.ds(g * G, G), :]).then_inc(wo_loaded, 16)
                    sp.wait_ge(wo_low, step * G + G)
                    load_qkv((g + 1) % NKV)
                for t in range(TILES):
                    sp.wait_ge(ring_emptied, ffn_task(base, TILES + t) + 1)
                    sp.dma_start(out_rows[bass.ds(half * HTOK + t * P, P), :], y[:, t, :]).then_inc(out_stored[t], 16)
                for t in range(TILES):
                    sp.wait_ge(out_stored[t], half * 16 + 16)
                sp.sem_inc(half_stored, 1)
            for t in range(TILES):
                sp.wait_ge(out_stored[t], 16 * HALVES)

        @block.gpsimd
        def _(pool):
            nc.gpsimd.memset(ident[:], 0.0).then_inc(ident_cleared, 1)
            pool.wait_ge(ident_cleared, 1)
            nc.gpsimd.affine_select(out=ident[:], in_=ident[:], compare_op=ALU.not_equal, fill=1.0, base=0,
                                    pattern=[[-1, P]], channel_multiplier=1).then_inc(ident_ready, 1)
            nc.gpsimd.memset(exponent[:], -0.5).then_inc(ident_ready, 1)
            for e in range(E):
                last = nc.gpsimd.memset(rev[:, e:e + 1], float(E - e))
            last.then_inc(ident_ready, 1)

            def split_qkv(step, c):
                pool.wait_ge(w_high, step * KC + c + 1)
                nc.gpsimd.tensor_tensor(w_l[:, c, :], raw[:, c, :], w_h[:, c, :].bitcast(F32),
                                        ALU.subtract).then_inc(w_low, 1)

            def split_wo(step):
                for h in range(G):
                    pool.wait_ge(wo_high, step * G + h + 1)
                    nc.gpsimd.tensor_tensor(wo_l[:, h, :], raw_o[:, h, :], wo_h[:, h, :].bitcast(F32),
                                            ALU.subtract).then_inc(wo_low, 1)

            def shift(U, c):
                blocks = slice(c * UB, (c + 1) * UB)
                pool.wait_ge(max_done, U * 2 + c + 1)
                nc.gpsimd.tensor_tensor(s[:, blocks, :], s[:, blocks, :],
                                        row_max[:, blocks].unsqueeze(2).broadcast_to([P, UB, L]),
                                        ALU.subtract).then_inc(shifted, 1)

            def normalise(U, c):
                blocks = slice(c * UB, (c + 1) * UB)
                pool.wait_ge(inv_done, U * 2 + c + 1)
                nc.gpsimd.tensor_tensor(s[:, blocks, :], s[:, blocks, :],
                                        row_inv[:, blocks].unsqueeze(2).broadcast_to([P, UB, L]),
                                        ALU.mult).then_inc(probs_ready, 1)

            def root(n, t0):
                pool.wait_ge(var_ready, n + 1)
                nc.gpsimd.tensor_tensor(rstd[:, t0:t0 + 4], rstd[:, t0:t0 + 4], exponent[:],
                                        ALU.pow).then_inc(rstd_ready, 1)

            pool.wait_ge(ident_ready, 3)
            for c in range(KC):
                split_qkv(0, c)
            with pool.Fori(0, HALVES) as half:
                root(half * 4, 0)
                root(half * 4 + 1, 4)
                for t in range(TILES):
                    pool.wait_ge(xn_ready, half * 2 * TILES + t + 1)
                    nc.gpsimd.tensor_tensor(y[:, t, :], y[:, t, :], bo_bc[:], ALU.add).then_inc(resid_ready, 1)
                with pool.Fori(0, NKV) as g:
                    step = half * NKV + g
                    for T in range(UNITS):
                        U = step * UNITS + T
                        shift(U, 0)
                        shift(U, 1)
                        if T == UNITS - 1:
                            split_qkv(step + 1, 0)
                        normalise(U, 0)
                        normalise(U, 1)
                        if T == 0:
                            split_wo(step)
                        else:
                            for c in range(1, KC):
                                split_qkv(step + 1, c)
                root(half * 4 + 2, 0)
                root(half * 4 + 3, 4)

        @block.scalar
        def _(act):
            def high(dst, src, bias_ap=None):
                if bias_ap is None:
                    return nc.scalar.activation(dst, src, ACT.Copy)
                return nc.scalar.activation(dst, src, ACT.Identity, bias=bias_ap)

            def split_qkv(step, c):
                if c == 0:
                    act.wait_ge(w_loaded, step * 48 + 48)
                high(w_h[:, c, :], raw[:, c, :]).then_inc(w_high, 1)

            for c in range(KC):
                split_qkv(0, c)
            act.wait_ge(ring_filled, 2)
            high(fw_h[:, :, 0:ER], ring[:, 1, :].rearrange("p (c n) -> p c n", c=KC)).then_inc(pro_high, 1)
            act.wait_ge(ring_filled, 3)
            high(fw_h[:, :, ER:FN], ring[:, 0, 0:KC * E].rearrange("p (c n) -> p c n", c=KC)).then_inc(pro_high, 1)
            act.wait_ge(ring_filled, 4)
            high(bm_h[:], ring[:, 1, :]).then_inc(pro_high, 1)
            act.wait_ge(ring_emptied, 1)

            def unit(base, g, step, T, first):
                U = step * UNITS + T
                u = g * UNITS + T
                act.wait_ge(bias_ready, step + 1)
                act.wait_ge(ring_filled, k_task(base, u, first) + 1)
                high(kT[:, :, 0, :], ring[:, 0, :].rearrange("p (b l) -> p b l", l=L),
                     g_bias[:, G:G + 1]).then_inc(qk_high, 1)
                for h in range(G):
                    act.wait_ge(ring_filled, q_task(base, u, first, h) + 1)
                    high(qT_h[:, :, h, :], ring[:, (1 + h) % 2, :].rearrange("p (b l) -> p b l", l=L), g_bias[:, h:h + 1]).then_inc(qk_high, 1)
                for c in range(2):
                    act.wait_ge(scores_filled, U * 4 + 2 * c + 2)
                    blocks = slice(c * UB, (c + 1) * UB)
                    act.copy(s_lo[:, blocks, :], att_s[:, blocks, 1, :]).then_inc(s_lo_copied, 1)
                for c in range(2):
                    act.wait_ge(v_turned, U * 2 + c + 1)
                    high(v_h[:, 4 * c:4 * c + 4, :], turn[:, c, :].rearrange("p (b d) -> p b d", d=HD)).then_inc(v_high, 1)
                for c in range(2):
                    blocks = slice(c * UB, (c + 1) * UB)
                    act.wait_ge(shifted, U * 2 + c + 1)
                    nc.scalar.activation(s[:, blocks, :], s[:, blocks, :], ACT.Exp, scale=ATT_SCALE).then_inc(exp_done, 1)
                    if T == UNITS - 1:
                        act.wait_ge(ring_filled, v_task(base, u, first) + 1)
                        split_qkv(step + 1, 2 * c)
                        split_qkv(step + 1, 2 * c + 1)
                for c in range(2):
                    act.wait_ge(p_turned, U * 2 + c + 1)
                    t_c = turn[:, c, :].rearrange("p (b q) -> p b q", q=P)
                    high(pT[0:L, 4 * c:4 * c + 4, 0, :], t_c[0:L])
                    high(pT[L:P, 4 * c:4 * c + 4, 1, :], t_c[L:P]).then_inc(p_high, 1)
                for j in range(4):
                    act.wait_ge(o_filled, U * 4 + j + 1)
                    high(oT_h.rearrange("p h (n b l) -> p n b h l", b=2, l=L)[:, j],
                         att_o[:, j]).then_inc(o_high, 1)
                if T == 0:
                    act.wait_ge(wo_loaded, step * 16 + 16)
                    if not first:
                        act.wait_ge(ring_filled, out_task(base, u, UT - 1) + 1)
                    for h in range(G):
                        high(wo_h[:, h, :], raw_o[:, h, :]).then_inc(wo_high, 1)

            with act.Fori(0, HALVES) as half:
                base = half * HALF_TASKS + PRO
                for t in range(2 * TILES):
                    act.wait_ge(ring_filled, base + t + 1)
                    dst = (cT_h if t < TILES else xT_h)[:, :, (t % TILES) * P:(t % TILES + 1) * P]
                    high(dst, ring[:, t % 2, :].rearrange("p (c n) -> p c n", c=KC)).then_inc(x_high, 1)
                unit(base, 0, half * NKV, 0, True)
                unit(base, 0, half * NKV, 1, False)
                with act.Fori(1, NKV) as g:
                    for T in range(UNITS):
                        unit(base, g, half * NKV + g, T, False)
                for t in range(TILES):
                    act.wait_ge(ring_filled, ffn_task(base, t) + 1)
                    high(fT_h[:, :, (t % 4) * P:(t % 4 + 1) * P],
                         ring[:, t % 2, :].rearrange("p (c n) -> p c n", c=KC)).then_inc(x_high, 1)
                act.wait_ge(gate_diff, half + 1)
                nc.scalar.activation(diff[:], diff[:], ACT.Exp).then_inc(gate_exp, 1)
                for c in range(2):
                    act.wait_ge(hw_turned, half * 2 + c + 1 + FREE)
                    high(hwT_h[:, c * 512:(c + 1) * 512], turn[:, c, :]).then_inc(hw_high, 1)

        @block.vector
        def _(dve):
            def low(dst, src, high_part):
                return nc.vector.tensor_tensor(dst, src, high_part.bitcast(F32), ALU.subtract)

            def low_biased(dst, src, bias_ap, high_part):
                return nc.vector.scalar_tensor_tensor(out=dst, in0=src, scalar=bias_ap, in1=high_part.bitcast(F32),
                                                      op0=ALU.add, op1=ALU.subtract)

            dve.wait_ge(ring_filled, 1)
            nc.vector.tensor_copy(bias[:, :, 0:G], ring[:, 0, 0:NH].rearrange("p (g h) -> p g h", h=G)).then_inc(o_low, FREE)
            nc.vector.tensor_copy(bias[:, :, G], ring[:, 0, NH:NH + NKV]).then_inc(p_low, FREE)
            nc.vector.tensor_copy(bias[:, :, G + 1], ring[:, 0, NH + NKV:NH + 2 * NKV]).then_inc(ring_emptied, 1)
            dve.wait_ge(pro_high, 1)
            low(fw_l[:, :, 0:ER], ring[:, 1, :].rearrange("p (c n) -> p c n", c=KC), fw_h[:, :, 0:ER]).then_inc(ring_emptied, 1)
            dve.wait_ge(pro_high, 2)
            low(fw_l[:, :, ER:FN], ring[:, 0, 0:KC * E].rearrange("p (c n) -> p c n", c=KC), fw_h[:, :, ER:FN]).then_inc(ring_emptied, 1)
            dve.wait_ge(pro_high, 3)
            low(bm_l[:], ring[:, 1, :], bm_h[:]).then_inc(ring_emptied, 1)
            dve.wait_ge(consts_loaded, 16 * N_CONSTS)
            dve.wait_ge(ident_ready, 3)

            def ln_stats(t, loaded=None):
                if loaded is not None:
                    dve.wait_ge(x_loaded[t], loaded)
                nc.vector.bn_stats(stats[:, t, :], y[:, t, :]).then_inc(ln_step, 1)

            def ln_scale(count, rooted, t0):
                dve.wait_ge(ln_step, count + 4)
                mean_e, mean_o = stats[:, t0:t0 + 4, 1], stats[:, t0:t0 + 4, 4]
                sq_e, sq_o = stats[:, t0:t0 + 4, 2], stats[:, t0:t0 + 4, 5]
                nc.vector.tensor_tensor(mean[:, t0:t0 + 4], mean_e, mean_o, ALU.add).then_inc(ln_step, 1)
                nc.vector.tensor_tensor(apart[:], mean_e, mean_o, ALU.subtract).then_inc(ln_step, 1)
                nc.vector.tensor_tensor(rstd[:, t0:t0 + 4], sq_e, sq_o, ALU.add).then_inc(ln_step, 1)
                dve.wait_ge(ln_step, count + 7)
                nc.vector.tensor_scalar(mean[:, t0:t0 + 4], mean[:, t0:t0 + 4], 0.5, None, ALU.mult).then_inc(ln_step, 1)
                nc.vector.tensor_tensor(apart[:], apart[:], apart[:], ALU.mult).then_inc(ln_step, 1)
                nc.vector.tensor_scalar(rstd[:, t0:t0 + 4], rstd[:, t0:t0 + 4], 1.0 / D, LN_EPS, ALU.mult,
                                        ALU.add).then_inc(ln_step, 1)
                dve.wait_ge(ln_step, count + 10)
                nc.vector.scalar_tensor_tensor(out=rstd[:, t0:t0 + 4], in0=apart[:], scalar=0.25, in1=rstd[:, t0:t0 + 4],
                                               op0=ALU.mult, op1=ALU.add).then_inc(var_ready, 1)
                dve.wait_ge(rstd_ready, rooted)

            def ln_tile(t, turned):
                if turned is not None:
                    dve.wait_ge(ring_filled, turned)
                nc.vector.tensor_scalar(xn[:, t % 2, :], y[:, t, :], mean[:, t:t + 1], rstd[:, t:t + 1],
                                        ALU.subtract, ALU.mult).then_inc(xn_ready, 1)

            LN_STEPS = 10

            def s_max(U, c):
                blocks = slice(c * UB, (c + 1) * UB)
                dve.wait_ge(s_lo_copied, U * 2 + c + 1)
                nc.vector.tensor_tensor(s[:, blocks, :], att_s[:, blocks, 0, :], s_lo[:, blocks, :], ALU.add).then_inc(s_added, 1)
                dve.wait_ge(s_added, U * 2 + c + 1)
                nc.vector.tensor_reduce(row_max[:, blocks], s[:, blocks, :], AX, ALU.max).then_inc(max_done, 1)

            def s_sum(U, c):
                blocks = slice(c * UB, (c + 1) * UB)
                dve.wait_ge(exp_done, U * 2 + c + 1)
                nc.vector.tensor_reduce(row_sum[:, blocks], s[:, blocks, :], AX, ALU.add).then_inc(sum_done, 1)
                dve.wait_ge(sum_done, U * 2 + c + 1)
                nc.vector.reciprocal(row_inv[:, blocks], row_sum[:, blocks]).then_inc(inv_done, 1)

            def out_add(base, u, T_prev, i):
                dve.wait_ge(ring_filled, out_task(base, u, i) + 1)
                t = T_prev * UT + i
                nc.vector.tensor_tensor(y[:, t, :], ring[:, i % 2, :], y[:, t, :], ALU.add).then_inc(ring_emptied, 1)

            def unit(base, g, step, T, first):
                U = step * UNITS + T
                u = g * UNITS + T
                if T == 0:
                    nc.vector.tensor_copy(g_bias[:], bias.rearrange("p g n -> p (g n)")[:, bass.ds(g * (G + 2), G + 2)]
                                          ).then_inc(bias_ready, 1)
                    dve.wait_ge(bias_ready, step + 1)
                dve.wait_ge(qk_high, U * (1 + G) + 1)
                low_biased(kT[:, :, 1, :], ring[:, 0, :].rearrange("p (b l) -> p b l", l=L),
                           g_bias[:, G:G + 1], kT[:, :, 0, :]).then_inc(ring_emptied, 1)
                for h in range(G):
                    dve.wait_ge(qk_high, U * (1 + G) + 2 + h)
                    low_biased(qT_l[:, :, h, :], ring[:, (1 + h) % 2, :].rearrange("p (b l) -> p b l", l=L),
                               g_bias[:, h:h + 1], qT_h[:, :, h, :]).then_inc(ring_emptied, 1)
                dve.wait_ge(ring_filled, v_task(base, u, first) + 1)
                nc.vector.tensor_scalar(vT[:], ring[:, 1, :].rearrange("p (b l) -> p b l", l=L).unsqueeze(2).broadcast_to([P, UB, 2, L]),
                                        g_bias[:, G + 1:G + 2], None, ALU.add).then_inc(ring_emptied, 1)
                s_max(U, 0)
                s_max(U, 1)
                for c in range(2):
                    dve.wait_ge(v_high, U * 2 + c + 1)
                    low(v_l[:, 4 * c:4 * c + 4, :], turn[:, c, :].rearrange("p (b d) -> p b d", d=HD),
                        v_h[:, 4 * c:4 * c + 4, :]).then_inc(v_low, 1)
                T_prev = (T + UNITS - 1) % UNITS
                if not first:
                    out_add(base, u, T_prev, 0)
                s_sum(U, 0)
                if not first:
                    out_add(base, u, T_prev, 1)
                s_sum(U, 1)
                if not first:
                    out_add(base, u, T_prev, 2)
                for c in range(2):
                    dve.wait_ge(p_high, U * 2 + c + 1)
                    t_c = turn[:, c, :].rearrange("p (b q) -> p b q", q=P)
                    b_c = slice(4 * c, 4 * c + 4)
                    low(pT[L:P, b_c, 0, :], t_c[0:L], pT[0:L, b_c, 0, :])
                    low(pT[0:L, b_c, 1, :], t_c[L:P], pT[L:P, b_c, 1, :]).then_inc(p_low, 1)
                if not first:
                    out_add(base, u, T_prev, 3)
                for j in range(4):
                    dve.wait_ge(o_high, U * 4 + j + 1)
                    o_view = lambda o: o.rearrange("p h (n b l) -> p n b h l", b=2, l=L)[:, j]
                    low(o_view(oT_l), att_o[:, j], o_view(oT_h)).then_inc(o_low, 1)

            with dve.Fori(0, HALVES) as half:
                base = half * HALF_TASKS + PRO
                ln0 = half * (4 * LN_STEPS)
                highs = half * (3 * TILES)
                loaded = half * 16 + 16

                def x_low(k, dst):
                    dve.wait_ge(x_high, highs + k + 1)
                    hi, lo = dst
                    low(lo, ring[:, k % 2, :].rearrange("p (c n) -> p c n", c=KC), hi).then_inc(ring_emptied, 1)

                def cols(pair, t):
                    return tuple(z[:, :, t * P:(t + 1) * P] for z in pair)

                for t in range(TILES):
                    x_low(t, cols((cT_h, cT_l), t))
                    ln_stats(t, loaded)
                    if t == 3:
                        ln_scale(ln0, half * 4 + 1, 0)
                        ln_tile(0, None)
                        ln_tile(1, None)
                ln_scale(ln0 + LN_STEPS, half * 4 + 2, 4)
                for t in range(TILES):
                    x_low(TILES + t, cols((xT_h, xT_l), t))
                    if t + 2 < TILES:
                        ln_tile(t + 2, base + TILES + t + 1)
                dve.wait_ge(resid_ready, half * TILES + TILES)
                unit(base, 0, half * NKV, 0, True)
                unit(base, 0, half * NKV, 1, False)
                with dve.Fori(1, NKV) as g:
                    for T in range(UNITS):
                        unit(base, g, half * NKV + g, T, False)

                dve.wait_ge(ring_emptied, out_task(base, NKV * UNITS - 1, UT - 1) + 1)
                for t in range(4):
                    ln_stats(t)
                ln_scale(ln0 + 2 * LN_STEPS, half * 4 + 3, 0)
                ln_tile(0, None)
                ln_tile(1, None)
                for i in range(UT):
                    out_add(base, NKV * UNITS, UNITS - 1, i)
                dve.wait_ge(ring_emptied, ffn_task(base, 0))
                for t in range(4, TILES):
                    ln_stats(t)
                ln_scale(ln0 + 3 * LN_STEPS, half * 4 + 4, 4)
                for t in range(TILES):
                    x_low_t = 2 * TILES + t
                    dve.wait_ge(x_high, highs + x_low_t + 1)
                    sl = slice((t % 4) * P, (t % 4 + 1) * P)
                    low(fT_l[:, :, sl], ring[:, t % 2, :].rearrange("p (c n) -> p c n", c=KC), fT_h[:, :, sl]).then_inc(ring_emptied, 1)
                    if t + 2 < TILES:
                        ln_tile(t + 2, ffn_task(base, t) + 1)

                steps = count(1)

                def chain(ins):
                    ins.then_inc(router_step, 1)
                    dve.wait_ge(router_step, half * ROUTER_STEPS + next(steps))

                def over(v):
                    return v.unsqueeze(2).broadcast_to([P, TILES, E])

                def first_max(values, peak, sel):
                    chain(nc.vector.tensor_reduce(peak[:], values[:], AX, ALU.max))
                    chain(nc.vector.tensor_tensor(mark[:], values[:], over(peak), ALU.is_ge))
                    chain(nc.vector.tensor_tensor(mark[:], mark[:], rev[:].unsqueeze(1).broadcast_to([P, TILES, E]), ALU.mult))
                    chain(nc.vector.tensor_reduce(top[:], mark[:], AX, ALU.max))
                    chain(nc.vector.tensor_tensor(sel[:], mark[:], over(top), ALU.is_equal))

                dve.wait_ge(experts_filled, half * TILES + TILES)
                chain(nc.vector.tensor_tensor(lg[:], att_f[:, :, ER:FN], rb_bc[:].unsqueeze(1).broadcast_to([P, TILES, E]), ALU.add))
                first_max(lg, m1, sel1)
                chain(nc.vector.scalar_tensor_tensor(out=lg2[:], in0=sel1[:], scalar=SKIP, in1=lg[:], op0=ALU.mult, op1=ALU.add))
                first_max(lg2, m2, sel2)
                nc.vector.tensor_tensor(diff[:], m2[:], m1[:], ALU.subtract).then_inc(gate_diff, 1)
                dve.wait_ge(gate_exp, half + 1)
                chain(nc.vector.tensor_scalar(top[:], diff[:], 1.0, 1.0 / LORA_SCALE, ALU.add, ALU.mult))
                chain(nc.vector.reciprocal(gate1[:], top[:]))
                chain(nc.vector.tensor_tensor(gate2[:], gate1[:], diff[:], ALU.mult))
                chain(nc.vector.tensor_tensor(sel1[:], sel1[:], over(gate1), ALU.mult))
                chain(nc.vector.tensor_tensor(sel2[:], sel2[:], over(gate2), ALU.mult))
                chain(nc.vector.tensor_tensor(sel1[:], sel1[:], sel2[:], ALU.add))
                for c in range(2):
                    ts = slice(4 * c, 4 * c + 4)
                    nc.vector.tensor_tensor(hw[:, ts, :].rearrange("p t (e r) -> p t e r", e=E),
                                            att_f[:, ts, 0:ER].rearrange("p t (e r) -> p t e r", e=E),
                                            sel1[:, ts, :].unsqueeze(3).broadcast_to([P, 4, E, R]),
                                            ALU.mult).then_inc(hw_ready, 1)
                for c in range(2):
                    dve.wait_ge(hw_high, half * 2 + c + 1)
                    low(hwT_l[:, c * 512:(c + 1) * 512], turn[:, c, :], hwT_h[:, c * 512:(c + 1) * 512]).then_inc(hw_low, 1)
                for t in range(TILES):
                    dve.wait_ge(ring_filled, ffn_task(base, TILES + t) + 1)
                    nc.vector.tensor_tensor(y[:, t, :], ring[:, t % 2, :], y[:, t, :], ALU.add).then_inc(ring_emptied, 1)

        @block.tensor
        def _(pe):
            mm = nc.tensor.matmul

            def passes(dst, stat, mov, start, stop):
                mm(dst, stat[0], mov[0], start=start, stop=False)
                mm(dst, stat[0], mov[1], start=False, stop=False)
                return mm(dst, stat[1], mov[0], start=False, stop=stop)

            pe.wait_ge(ident_ready, 3)
            pe.wait_ge(consts_loaded, 16 * N_CONSTS)
            nb = NH + 2 * NKV
            nc.tensor.transpose(ring[:, 0, 0:nb], bias_rows[:], ident[0:nb, 0:nb]).then_inc(ring_filled, 1)
            for c in range(KC):
                last = nc.tensor.transpose(ring[:, 1, c * P:(c + 1) * P], xn[:, 0, c * P:(c + 1) * P], ident[:])
                if c == 0:
                    last.then_inc(hw_turned, FREE)
            last.then_inc(ring_filled, 1)
            pe.wait_ge(ring_emptied, 1)
            for c in range(KC):
                last = nc.tensor.transpose(ring[:, 0, c * E:(c + 1) * E], xn[0:E, 1, c * P:(c + 1) * P], ident[0:E, 0:E])
            last.then_inc(ring_filled, 1)
            pe.wait_ge(ring_emptied, 2)
            for c in range(KC):
                last = nc.tensor.transpose(ring[:, 1, c * P:(c + 1) * P], c_stage[:, 0, c * P:(c + 1) * P], ident[:])
            last.then_inc(ring_filled, 1)

            def turn_tile(n, slot, src):
                pe.wait_ge(ring_emptied, n - 1)
                for c in range(KC):
                    last = nc.tensor.transpose(ring[:, slot, c * P:(c + 1) * P], src[:, c * P:(c + 1) * P], ident[:])
                last.then_inc(ring_filled, 1)

            def project(n, slot, cols, xT, tok, step=None):
                pe.wait_ge(ring_emptied, n - 1)
                for c in range(KC):
                    if step is not None:
                        pe.wait_ge(w_low, step * KC + c + 1)
                    last = passes(ring[:, slot, :], (w_h[:, c, cols], w_l[:, c, cols]),
                                  (xT[0][:, c, tok], xT[1][:, c, tok]), c == 0, c == KC - 1)
                last.then_inc(ring_filled, 1)

            def out_project(base, u, i):
                pe.wait_ge(ring_emptied, out_task(base, u, i) - 1)
                tok = slice(i * P, (i + 1) * P)
                for h in range(G):
                    last = passes(ring[:, i % 2, :], (oT_h[:, h, tok], oT_l[:, h, tok]),
                                  (wo_h[:, h, :], wo_l[:, h, :]), h == 0, h == G - 1)
                last.then_inc(ring_filled, 1)

            def unit(base, g, step, T, first):
                U = step * UNITS + T
                u = g * UNITS + T
                tok = slice(T * UTOK, (T + 1) * UTOK)
                project(k_task(base, u, first), 0, slice(G * HD, G * HD + HD), (cT_h, cT_l), tok, step if T == 0 else None)
                for h in range(G):
                    project(q_task(base, u, first, h), (1 + h) % 2, slice(h * HD, (h + 1) * HD), (xT_h, xT_l), tok)
                project(v_task(base, u, first), 1, slice(G * HD + HD, QKV), (cT_h, cT_l), tok)
                pe.wait_ge(ring_emptied, v_task(base, u, first))
                pe.wait_ge(o_low, U * 4 + FREE)
                for b in range(UB):
                    for hp in range(HP):
                        dst = att[:, b // 2, (b % 2) * 256 + hp * P:(b % 2) * 256 + (hp + 1) * P]
                        q_h, q_l = (q[:, b, 2 * hp:2 * hp + 2, :].rearrange("p h l -> p (h l)") for q in (qT_h, qT_l))
                        keys = kT[:, b, :, :].rearrange("p k l -> p (k l)")
                        mm(dst, q_h, keys, start=True, stop=False)
                        last = mm(dst, q_l, keys, start=False, stop=True)
                    if b % 2:
                        last.then_inc(scores_filled, 1)
                pe.wait_ge(ring_emptied, v_task(base, u, first) + 1)
                for c in range(2):
                    pe.wait_ge(p_low, U * 2 + FREE)
                    for b in range(4 * c, 4 * c + 4):
                        last = nc.tensor.transpose(turn[:, c, (b % 4) * HD:(b % 4 + 1) * HD],
                                                   vT[:, b, :, :].rearrange("p k l -> p (k l)"), ident[:])
                    last.then_inc(v_turned, 1)
                if not first:
                    if T == 1:
                        pe.wait_ge(wo_low, step * G + G)
                    for i in range(UT - 1):
                        out_project(base, u, i)
                for c in range(2):
                    pe.wait_ge(probs_ready, U * 2 + c + 1)
                    pe.wait_ge(v_low, U * 2 + c + 1)
                    for b in range(4 * c, 4 * c + 4):
                        last = nc.tensor.transpose(turn[:, c, (b % 4) * P:(b % 4 + 1) * P],
                                                   s[:, HP * b:HP * b + HP, :].rearrange("p k l -> p (k l)"), ident[:])
                    last.then_inc(p_turned, 1)
                if not first:
                    out_project(base, u, UT - 1)
                for b in range(UB):
                    if b % 4 == 0:
                        pe.wait_ge(p_low, U * 2 + b // 4 + 1 + FREE)
                    dst = att[:, b // 2, (b % 2) * 256:(b % 2 + 1) * 256]
                    probs = pT[:, b, :, :].rearrange("p k l -> p (k l)")
                    mm(dst, v_h[:, b, :], probs, start=True, stop=False)
                    last = mm(dst, v_l[:, b, :], probs, start=False, stop=True)
                    if b % 2:
                        last.then_inc(o_filled, 1)

            with pe.Fori(0, HALVES) as half:
                base = half * HALF_TASKS + PRO
                for t in range(TILES):
                    pe.wait_ge(c_loaded[t % 4], half * 32 + 16 * (t // 4) + 16)
                    turn_tile(base + t, t % 2, c_stage[:, t % 4, :])
                for t in range(TILES):
                    pe.wait_ge(xn_ready, half * 2 * TILES + t + 1)
                    turn_tile(base + TILES + t, t % 2, xn[:, t % 2, :])
                pe.wait_ge(ring_emptied, base + 2 * TILES)
                unit(base, 0, half * NKV, 0, True)
                unit(base, 0, half * NKV, 1, False)
                with pe.Fori(1, NKV) as g:
                    for T in range(UNITS):
                        unit(base, g, half * NKV + g, T, False)
                pe.wait_ge(o_low, half * (NKV * UNITS * 4) + NKV * UNITS * 4 + FREE)
                for i in range(UT):
                    out_project(base, NKV * UNITS, i)

                def down(t):
                    pe.wait_ge(ring_emptied, ffn_task(base, t) + 1)
                    sl = slice((t % 4) * P, (t % 4 + 1) * P)
                    for c in range(KC):
                        last = passes(att_f[:, t, 0:FN], (fT_h[:, c, sl], fT_l[:, c, sl]),
                                      (fw_h[:, c, :], fw_l[:, c, :]), c == 0, c == KC - 1)
                    last.then_inc(experts_filled, 1)

                for t in range(TILES):
                    pe.wait_ge(xn_ready, half * 2 * TILES + TILES + t + 1)
                    turn_tile(ffn_task(base, t), t % 2, xn[:, t % 2, :])
                    if t >= 1:
                        down(t - 1)
                down(TILES - 1)
                for c in range(2):
                    pe.wait_ge(hw_ready, half * 2 + c + 1)
                    for t in range(4 * c, 4 * c + 4):
                        last = nc.tensor.transpose(turn[:, c, (t % 4) * P:(t % 4 + 1) * P], hw[:, t, :], ident[:])
                    last.then_inc(hw_turned, 1)
                for t in range(TILES):
                    if t % 4 == 0:
                        pe.wait_ge(hw_low, half * 2 + t // 4 + 1)
                    pe.wait_ge(ring_emptied, ffn_task(base, TILES + t) - 1)
                    sl = slice(t * P, (t + 1) * P)
                    passes(ring[:, t % 2, :], (hwT_h[:, sl], hwT_l[:, sl]), (bm_h[:], bm_l[:]),
                           True, True).then_inc(ring_filled, 1)


_INS = ["x", "ctx_4096", "L0_xattn_Wq", "L0_xattn_bq", "L0_xattn_Wkv", "L0_xattn_bkv", "L0_xattn_Wo", "L0_xattn_bo",
        "L0_ffn_router_w", "L0_ffn_router_b", "L0_ffn_A", "L0_ffn_Bm"]


def kernel(**inputs):
    import numpy as _np
    import concourse.bacc as _bacc
    from concourse import mybir as _mybir
    from concourse.bass_utils import run_bass_kernel_spmd as _run

    nc = _bacc.Bacc("TRN2", target_bir_lowering=False, num_devices=1)
    arrays, args = {}, []
    for name in _INS:
        a = _np.ascontiguousarray(inputs[name])
        arrays[f"in_{name}_dram"] = a
        args.append(nc.dram_tensor(f"in_{name}_dram", a.shape, _mybir.dt.from_np(a.dtype), kind="ExternalInput").ap())
    args.append(nc.dram_tensor("out_dram", (B, L, D), F32, kind="ExternalOutput").ap())
    build(nc, *args)
    r = _run(nc, [arrays], core_ids=[0])
    return r.results[0]["out_dram"]
```

```python
from contextlib import ExitStack
from itertools import count

import concourse.bass as bass
import concourse.mybir as mybir

F32 = mybir.dt.float32
F32R = mybir.dt.float32r
ACT = mybir.ActivationFunctionType
ALU = mybir.AluOpType
AX = mybir.AxisListType.X

P = 128
B, L, D = 32, 64, 512
NH, NKV, HD = 32, 8, 128
G = NH // NKV
KC = D // P
TOK = B * L
TILES = TOK // P
UTOK = 512
UNITS = TOK // UTOK
NU = NKV * UNITS
UB = UTOK // L
UT = UTOK // P
HP = G // 2
KVH = D // HD
CHUNKS = 2 * NKV // KVH // 2
PARTS = 2
PTILES = TILES // PARTS
STEPS = PARTS * CHUNKS
E, R = 8, 16
ER = E * R
FN = ER + E
ETILES = 8
EBATCHES = TILES // ETILES
ATT_SCALE = 1.0 / float(HD) ** 0.5
LN_EPS = 1e-5
LORA_SCALE = 8.0 / R
SKIP = -3.0e38
SLOTS = 3
LN_STEPS = 10
UNIT_TASKS = G + UT


def task_order():
    start = [("c", 0), ("c", 1), ("c", 2), ("c", 3), ("bias",)]
    for j in range(STEPS):
        part, chunk = j // CHUNKS, j % CHUNKS
        for t in range(PTILES):
            start.append(("V", j, t))
            if chunk == 0 and t < 4:
                start.append(("c", part * PTILES + 4 + t))
            if t >= 4:
                start.append(("x", 4 * j + t - 4))
        for b in range(PTILES // 4):
            for k in range(KVH):
                start.append(("K", j, b, k))
                if b == 1 and chunk == CHUNKS - 1 and part + 1 < PARTS:
                    start.append(("c", (part + 1) * PTILES + k))
    tail = [("W", 0), ("W", 1), ("W", 2), ("W", 3), ("A",), ("router",), ("Bm",)]
    tail += [("f", t) for t in range(TILES)] + [("e", t) for t in range(TILES)]
    return start, tail


def vector_order(start, tail):
    after = {}
    for j in range(STEPS):
        after["V", j, 1] = [("S", "x", 4 * j)]
        after["V", j, 3] = [("n", "x", 4 * j), ("n", "x", 4 * j + 1)]
        if j % CHUNKS == 0:
            after["c", j // CHUNKS * PTILES + 7] = after.pop(("V", j, 3))
        after["x", 4 * j] = [("n", "x", 4 * j + 2)]
        after["x", 4 * j + 1] = [("n", "x", 4 * j + 3)]
    after["W", 0] = [("S", "f", 0)]
    after["W", 1] = [("n", "f", 0), ("n", "f", 1)]
    after["W", 2] = [("S", "f", 4)]
    for t in range(TILES - 2):
        after["f", t] = [("n", "f", t + 2)]
    after["f", 3].append(("S", "f", 8))
    after["f", 7].append(("S", "f", 12))
    steps = [[], []]
    for which, names in enumerate((start, tail)):
        for name in names:
            steps[which] += [name] + after.get(name, [])
    return steps


def build(nc, x, ctx_in, wq, bq, wkv, bkv, wo, bo, router_w, router_b, A, Bm, out, keys_dram, values_dram):
    ctx = ExitStack()
    with ctx:
        def sb(name, shape, dt=F32):
            return ctx.enter_context(nc.sbuf_tensor(name, shape, dt))

        def sem(name):
            return ctx.enter_context(nc.semaphore(name))

        x_rows = x.rearrange("b l d -> (b l) d")
        c_rows = ctx_in.rearrange("b l d -> (b l) d")
        out_rows = out.rearrange("b l d -> (b l) d")
        wq_v = wq.rearrange("(c p) n -> p c n", p=P)
        wkv_v = wkv.rearrange("(c p) n -> p c n", p=P)
        wo_v = wo.rearrange("(h p) n -> p h n", p=P)
        values_v = values_dram.rearrange("(g k) (b d) -> k g b d", k=L, d=HD)

        ident = sb("ident", [P, P])
        bias = sb("bias", [P, NH + NKV])
        g_bias = sb("g_bias", [P, G])
        rb_bc = sb("rb_bc", [P, E])
        rev = sb("rev", [P, E])
        y = sb("y", [P, TILES, D])
        c_stage, bias_rows = y[:, TILES - PTILES:TILES, :], y[0:NH + NKV, TILES - PTILES - 1, 0:HD]
        xT_h, xT_l = sb("xT_h", [P, KC, TOK], F32R), sb("xT_l", [P, KC, TOK], F32R)
        w_h, w_l = sb("w_h", [P, KC, D], F32R), sb("w_l", [P, KC, D], F32R)
        wo_h, wo_l = sb("wo_h", [P, G, D], F32R), sb("wo_l", [P, G, D], F32R)
        raw = sb("raw", [P, KC, D])
        a_rows, bm_rows, router_rows = raw[:, 0, :], raw[:, 1, :], raw[0:E, 2, :]
        qT_h, qT_l = sb("qT_h", [P, UB, G, L], F32R), sb("qT_l", [P, UB, G, L], F32R)
        oT_h, oT_l = sb("oT_h", [P, G, UTOK], F32R), sb("oT_l", [P, G, UTOK], F32R)
        cT = [tuple(q.rearrange("p b h l -> p (b h l)").rearrange("p (c n) -> p c n", c=KC) for q in (qT_h, qT_l)),
              (oT_h, oT_l)]
        (fw_h, bm_h), (fw_l, bm_l) = (
            (m[:, 0:KC * FN].rearrange("p (c n) -> p c n", c=KC), m[:, KC * FN:KC * FN + D])
            for m in (q.rearrange("p b h l -> p (b h l)") for q in (qT_h, qT_l)))
        k_raw = sb("k_raw", [P, UB, L])
        kT = sb("kT", [P, 2, UB, L], F32R)
        v_raw = sb("v_raw", [P, UB, HD])
        v_h, v_l = sb("v_h", [P, UB, HD], F32R), sb("v_l", [P, UB, HD], F32R)
        bv_bc, bo_bc = v_raw.rearrange("p b d -> p (b d)"), k_raw.rearrange("p b l -> p (b l)")
        s_mem = sb("s_mem", [P, SLOTS * D])
        kv_stage = s_mem.rearrange("p (t d) -> p t d", d=D)
        s = s_mem[:, 0:2 * D].rearrange("p (n l) -> p n l", l=L)
        hw = s_mem[:, 0:2 * D].rearrange("p (t n) -> p t n", n=ER)
        lg, lg2, sel1, sel2, mark = (
            s_mem[:, 2 * D + i * ETILES * E:2 * D + (i + 1) * ETILES * E].rearrange("p (t e) -> p t e", e=E)
            for i in range(5))
        m1, m2, top, diff, gate1, gate2 = (
            s_mem[:, 2 * D + 5 * ETILES * E + i * ETILES:2 * D + 5 * ETILES * E + (i + 1) * ETILES] for i in range(6))
        low_or_x = sb("low_or_x", [P, 2 * D])
        s_lo = low_or_x.rearrange("p (n l) -> p n l", l=L)
        xn = low_or_x.rearrange("p (t d) -> p t d", d=D)
        row_max = sb("row_max", [P, UB * HP])
        row_sum = sb("row_sum", [P, UB * HP])
        row_inv = sb("row_inv", [P, UB * HP])
        pT = sb("pT", [P, UB, HP, P], F32R)
        stats = sb("stats", [P, TILES, 6])
        mean, apart = sb("mean", [P, TILES]), sb("apart", [P, 4])
        rstd = sb("rstd", [P, TILES])
        exponent = sb("exponent", [P, 4])
        hwT_h, hwT_l = (o.rearrange("p h n -> p (h n)")[:, 0:ETILES * P] for o in (oT_h, oT_l))

        ring = ctx.enter_context(nc.psum_tensor("ring", [P, 2, 512], F32))
        att = ctx.enter_context(nc.psum_tensor("att", [P, 4, 512], F32))
        turn = ctx.enter_context(nc.psum_tensor("turn", [P, 2, 512], F32))
        att_s = att.rearrange("p n (b k l) -> p (n b) k l", k=2, l=L)
        att_o = att.rearrange("p n (b h l) -> p n b h l", b=2, h=G)
        att_f = att.rearrange("p n (t f) -> p (n t) f", t=2)

        bias_loaded, small_loaded, bc_loaded = sem("bias_loaded"), sem("small_loaded"), sem("bc_loaded")
        ident_cleared, ident_ready, const_ready = sem("ident_cleared"), sem("ident_ready"), sem("const_ready")
        w_loaded, wo_loaded, k_loaded, v_loaded = sem("w_loaded"), sem("wo_loaded"), sem("k_loaded"), sem("v_loaded")
        x_loaded = [sem(f"x_loaded{t}") for t in range(TILES)]
        c_loaded = [sem(f"c_loaded{t}") for t in range(PTILES)]
        kv_stored = [sem(f"kv_stored{t}") for t in range(SLOTS)]
        out_stored = sem("out_stored")
        ring_filled, tile_filled, scores_filled = sem("ring_filled"), sem("tile_filled"), sem("scores_filled")
        p_turned, o_filled = sem("p_turned"), sem("o_filled")
        experts_filled, hw_turned = sem("experts_filled"), sem("hw_turned")
        small_high, x_high, q_high, k_high = sem("small_high"), sem("x_high"), sem("q_high"), sem("k_high")
        s_lo_copied, exp_done = sem("s_lo_copied"), sem("exp_done")
        v_high, p_high, o_high = sem("v_high"), sem("p_high"), sem("o_high")
        w_high, wo_high = sem("w_high"), sem("wo_high")
        gate_exp, hw_high = sem("gate_exp"), sem("hw_high")
        ring_emptied, tile_emptied = sem("ring_emptied"), sem("tile_emptied")
        s_added, max_done = sem("s_added"), sem("max_done")
        sum_done, inv_done = sem("sum_done"), sem("inv_done")
        p_low, o_low, hw_low = sem("p_low"), sem("o_low"), sem("hw_low")
        ln_step, xn_ready, router_step, hw_ready = sem("ln_step"), sem("xn_ready"), sem("router_step"), sem("hw_ready")
        bias_ready, gate_diff, var_ready = sem("bias_ready"), sem("gate_diff"), sem("var_ready")
        shifted, probs_ready, w_low, wo_low = sem("shifted"), sem("probs_ready"), sem("w_low"), sem("wo_low")
        k_low, v_low, resid_ready, rstd_ready = sem("k_low"), sem("v_low"), sem("resid_ready"), sem("rstd_ready")

        START, TAIL = task_order()
        START_V, TAIL_V = vector_order(START, TAIL)
        ring_start, ring_tail = ([name for name in names if name[0] not in "cxf"] for names in (START, TAIL))
        pos = {name: n for n, name in enumerate(ring_start)}
        FIRST_UNIT = len(ring_start)
        TAIL_TASKS = FIRST_UNIT + G + UNIT_TASKS * (NU - 1)
        pos.update({name: TAIL_TASKS + n for n, name in enumerate(ring_tail)})

        def q_task(u, h):
            return FIRST_UNIT + h if isinstance(u, int) and u == 0 else FIRST_UNIT + G + UNIT_TASKS * (u - 1) + h

        def out_task(u, i):
            return FIRST_UNIT + G + UNIT_TASKS * (u - 1) + G + i

        def q_slot(u, h):
            return (FIRST_UNIT + h) % 2

        def out_slot(i):
            return out_task(1, i) % 2

        tile_no = {name: n for n, name in enumerate(name for name in START + TAIL if name[0] in "cxf")}
        norm_order = [name for name in START + TAIL if name[0] in "xf"]
        norm_no = {name: n for n, name in enumerate(norm_order)}
        batches = [("x", t) for t in range(0, TILES, 4)] + [("f", t) for t in range(0, TILES, 4)]
        kv_order = [name for name in START if name[0] in "KV"]
        kv_no = {name: m for m, name in enumerate(kv_order)}
        kv_value = []
        for m, name in enumerate(kv_order):
            kv_value.append((kv_value[m - SLOTS] if m >= SLOTS else 0) + (32 if name[0] == "V" else 16))

        def turned_tile(name):
            kind, t = name
            if kind != "c":
                return xT_h[:, :, t * P:(t + 1) * P], xT_l[:, :, t * P:(t + 1) * P]
            return tuple(part[:, :, (t % 4) * P:(t % 4 + 1) * P] for part in cT[t % PTILES // 4])

        block = ctx.enter_context(nc.Block())

        @block.sync
        def _(sp):
            def load_w(step, src, col):
                if not isinstance(step, int) or step > 0:
                    sp.wait_ge(wo_low, step * KC)
                sp.dma_start(raw[:], src[:, :, bass.ds(col, D)]).then_inc(w_loaded, 16)

            def load_wo(step, src):
                sp.wait_ge(w_low, step * KC + KC)
                sp.dma_start(raw[:], src).then_inc(wo_loaded, 16)

            def load_c(t):
                if t >= PTILES:
                    sp.wait_ge(tile_filled, tile_no["c", t - PTILES] + 1)
                sp.dma_start(c_stage[:, t % PTILES, :], c_rows[t * P:(t + 1) * P, :]).then_inc(c_loaded[t % PTILES], 16)

            def load_x(t):
                sp.dma_start(y[:, t, :], x_rows[t * P:(t + 1) * P, :]).then_inc(x_loaded[t], 16)

            def store_kv(name):
                m = kv_no[name]
                sp.wait_ge(ring_emptied, pos[name] + 1)
                part, chunk = name[1] // CHUNKS, name[1] % CHUNKS
                if name[0] == "V":
                    for i in range(2):
                        sp.dma_start(values_v[:, chunk * KVH:(chunk + 1) * KVH, 2 * (part * PTILES + name[2]) + i, :],
                                     kv_stage[i * L:(i + 1) * L, m % SLOTS, :].rearrange("p (g d) -> p g d", d=HD)
                                     ).then_inc(kv_stored[m % SLOTS], 16)
                else:
                    r0, c0 = (chunk * KVH + name[3]) * HD, (part * (PTILES // 4) + name[2]) * UTOK
                    sp.dma_start(keys_dram[r0:r0 + HD, c0:c0 + UTOK], kv_stage[:, m % SLOTS, :]).then_inc(kv_stored[m % SLOTS], 16)

            def values_weights(step):
                load_w(step, wkv_v, NKV * HD + step % CHUNKS * D)

            for t in range(4):
                load_c(t)
            values_weights(0)
            sp.dma_start(bias_rows[0:NH, :], bq.rearrange("(h p) -> h p", p=HD)).then_inc(bias_loaded, 16)
            sp.dma_start(bias_rows[NH:NH + NKV, :], bkv[0:NKV * HD].rearrange("(h p) -> h p", p=HD)).then_inc(bias_loaded, 16)
            sp.dma_start(bv_bc, bkv[NKV * HD:2 * NKV * HD].rearrange("(a d) -> a d", a=1).broadcast_to([P, NKV * HD])
                         ).then_inc(bias_loaded, 16)
            for t in range(4, 8):
                load_c(t)
            for t in range(4):
                load_x(t)
            sp.dma_start(bo_bc, bo.rearrange("(a d) -> a d", a=1).broadcast_to([P, D])).then_inc(bc_loaded, 16)
            sp.dma_start(rb_bc[:], router_b.rearrange("(a d) -> a d", a=1).broadcast_to([P, E])).then_inc(bc_loaded, 16)
            for name in START:
                if name[0] in "KV":
                    if name[0] == "V" and name[2] == 0:
                        load_wo(name[1], wkv_v[:, :, name[1] % CHUNKS * D:(name[1] % CHUNKS + 1) * D])
                    if name == ("V", 0, 0):
                        sp.wait_ge(ring_filled, pos["bias",] + 1)
                        for t in range(4, TILES - PTILES):
                            load_x(t)
                    store_kv(name)
                    if name[0] == "K" and name[2:] == (0, 1):
                        if name[1] + 1 < STEPS:
                            values_weights(name[1] + 1)
                        else:
                            load_w(STEPS, wq_v, 0)
                if name[0] == "c" and 4 <= name[1] < PTILES:
                    load_c(name[1] + 4)
                    if name[1] == PTILES - 1:
                        for t in range(PTILES + 4, TILES):
                            load_c(t)
                if name in (("K", 1, 1, 3), ("V", 2, 4)):
                    last = 11 if name[0] == "K" else 15
                    sp.wait_ge(tile_filled, tile_no["c", last] + 1)
                    for t in range(last - 3, last + 1):
                        load_x(t)

            def unit(g, T, first):
                step, u = STEPS + g, g * UNITS + T
                if first:
                    for m in range(len(kv_order) - SLOTS, len(kv_order)):
                        sp.wait_ge(kv_stored[m % SLOTS], kv_value[m])
                    sp.wait_ge(resid_ready, TILES)
                else:
                    sp.wait_ge(scores_filled, u * UB // 2)
                sp.dma_start(k_raw.rearrange("p b l -> p (b l)"),
                             keys_dram[bass.ds(g * HD, HD), T * UTOK:(T + 1) * UTOK]).then_inc(k_loaded, 16)
                if T == 0:
                    load_wo(step, wo_v[:, bass.ds(g * G, G), :])
                if T == 2:
                    load_w(step + 1, wq_v, (g + 1) % NKV * (G * HD))
                if not first:
                    sp.wait_ge(o_filled, u * UB // 2)
                for i in range(2):
                    sp.dma_start(v_raw[i * L:(i + 1) * L].rearrange("p b d -> p (b d)"),
                                 values_dram[bass.ds(g * L, L), T * UB * HD:(T + 1) * UB * HD]).then_inc(v_loaded, 16)

            unit(0, 0, True)
            for T in range(1, UNITS):
                unit(0, T, False)
            with sp.Fori(1, NKV) as g:
                for T in range(UNITS):
                    unit(g, T, False)
            sp.wait_ge(w_low, (STEPS + NKV) * KC + KC)
            sp.dma_start(a_rows, A.rearrange("e r d -> (e r) d")).then_inc(small_loaded, 16)
            sp.dma_start(router_rows, router_w).then_inc(small_loaded, 16)
            for c in range(KC):
                sp.dma_start(bm_rows.rearrange("p (c e r) -> p c e r", c=KC, e=E)[:, c],
                             Bm[:, c * P:(c + 1) * P, :].rearrange("e p r -> p e r")).then_inc(small_loaded, 16)
            for t in range(TILES):
                sp.wait_ge(ring_emptied, pos["e", t] + 1)
                sp.dma_start(out_rows[t * P:(t + 1) * P, :], y[:, t, :]).then_inc(out_stored, 16)
            sp.wait_ge(out_stored, 16 * TILES)
            sp.wait_ge(w_loaded, 16 * (STEPS + NKV + 1))

        @block.gpsimd
        def _(pool):
            nc.gpsimd.memset(ident[:], 0.0).then_inc(ident_cleared, 1)
            pool.wait_ge(ident_cleared, 1)
            nc.gpsimd.affine_select(out=ident[:], in_=ident[:], compare_op=ALU.not_equal, fill=1.0, base=0,
                                    pattern=[[-1, P]], channel_multiplier=1).then_inc(ident_ready, 1)
            nc.gpsimd.memset(exponent[:], -0.5).then_inc(const_ready, 1)
            for e in range(E):
                last = nc.gpsimd.memset(rev[:, e:e + 1], float(E - e))
            last.then_inc(const_ready, 1)
            pool.wait_ge(const_ready, 2)

            def low(dst, src, high_part):
                return nc.gpsimd.tensor_tensor(dst, src, high_part.bitcast(F32), ALU.subtract)

            def split_w(step, c):
                pool.wait_ge(w_high, step * KC + c + 1)
                low(w_l[:, c, :], raw[:, c, :], w_h[:, c, :]).then_inc(w_low, 1)

            def split_wo(step):
                for c in range(KC):
                    pool.wait_ge(wo_high, step * KC + c + 1)
                    low(wo_l[:, c, :], raw[:, c, :], wo_h[:, c, :]).then_inc(wo_low, 1)

            def shift(u, c):
                blocks = slice(c * UB, (c + 1) * UB)
                pool.wait_ge(max_done, u * 2 + c + 1)
                nc.gpsimd.tensor_tensor(s[:, blocks, :], s[:, blocks, :],
                                        row_max[:, blocks].unsqueeze(2).broadcast_to([P, UB, L]),
                                        ALU.subtract).then_inc(shifted, 1)

            def normalise(u, c):
                blocks = slice(c * UB, (c + 1) * UB)
                pool.wait_ge(inv_done, u * 2 + c + 1)
                nc.gpsimd.tensor_tensor(s[:, blocks, :], s[:, blocks, :],
                                        row_inv[:, blocks].unsqueeze(2).broadcast_to([P, UB, L]),
                                        ALU.mult).then_inc(probs_ready, 1)

            def root(kind, t0):
                pool.wait_ge(var_ready, batches.index((kind, t0)) + 1)
                nc.gpsimd.tensor_tensor(rstd[:, t0:t0 + 4], rstd[:, t0:t0 + 4], exponent[:],
                                        ALU.pow).then_inc(rstd_ready, 1)

            def unit(g, T, first):
                step, u = STEPS + g, g * UNITS + T
                if T == 1:
                    split_wo(step)
                pool.wait_ge(k_high, u + 1)
                low(kT[:, 1], k_raw[:], kT[:, 0]).then_inc(k_low, 1)
                pool.wait_ge(v_high, u + 1)
                low(v_l[:], v_raw[:], v_h[:]).then_inc(v_low, 1)
                shift(u, 0)
                shift(u, 1)
                if T == UNITS - 1:
                    split_w(step + 1, 0)
                normalise(u, 0)
                normalise(u, 1)
                if T == UNITS - 1:
                    for c in range(1, KC):
                        split_w(step + 1, c)

            for c in range(KC):
                split_w(0, c)
            for j in range(STEPS):
                root("x", 4 * j)
                split_wo(j)
                if j == 0:
                    pool.wait_ge(bc_loaded, 32)
                for t in range(4 * j, 4 * j + 4):
                    pool.wait_ge(xn_ready, norm_no["x", t] + 1)
                    nc.gpsimd.tensor_tensor(y[:, t, :], y[:, t, :], bo_bc, ALU.add).then_inc(resid_ready, 1)
                for c in range(KC):
                    split_w(j + 1, c)
            unit(0, 0, True)
            for T in range(1, UNITS):
                unit(0, T, False)
            with pool.Fori(1, NKV) as g:
                for T in range(UNITS):
                    unit(g, T, False)
            for t in range(0, TILES, 4):
                root("f", t)

        @block.scalar
        def _(act):
            def high(dst, src, bias_ap=None):
                if bias_ap is None:
                    return nc.scalar.activation(dst, src, ACT.Copy)
                return nc.scalar.activation(dst, src, ACT.Identity, bias=bias_ap)

            def split_w(step, c):
                if c == 0:
                    act.wait_ge(w_loaded, step * 16 + 16)
                high(w_h[:, c, :], raw[:, c, :]).then_inc(w_high, 1)

            def split_wo(step):
                act.wait_ge(wo_loaded, step * 16 + 16)
                for c in range(KC):
                    high(wo_h[:, c, :], raw[:, c, :]).then_inc(wo_high, 1)

            def tile_high(name):
                n = tile_no[name]
                act.wait_ge(tile_filled, n + 1)
                high(turned_tile(name)[0], turn[:, n % 2, :].rearrange("p (c n) -> p c n", c=KC)).then_inc(x_high, 1)

            def query_high(u, h):
                act.wait_ge(ring_filled, q_task(u, h) + 1)
                high(qT_h[:, :, h, :], ring[:, q_slot(u, h), :].rearrange("p (b l) -> p b l", l=L),
                     g_bias[:, h:h + 1]).then_inc(q_high, 1)

            def probs_high(u):
                for c in range(2):
                    act.wait_ge(p_turned, u * 2 - 1 + c)
                    t_c = turn[:, c, :].rearrange("p (b q) -> p b q", q=P)
                    high(pT[0:L, 4 * c:4 * c + 4, 0, :], t_c[0:L])
                    high(pT[L:P, 4 * c:4 * c + 4, 1, :], t_c[L:P]).then_inc(p_high, 1)

            def outputs_high(u):
                for j in range(4):
                    act.wait_ge(o_filled, u * 4 - 3 + j)
                    high(oT_h.rearrange("p h (n b l) -> p n b h l", b=2, l=L)[:, j], att_o[:, j]).then_inc(o_high, 1)

            def unit(g, T, first):
                step, u = STEPS + g, g * UNITS + T
                if not first:
                    probs_high(u)
                if T == 0:
                    act.wait_ge(bias_ready, g + 1)
                query_high(u, 0)
                if T == 1:
                    if not (isinstance(u, int) and u == 1):
                        act.wait_ge(ring_filled, out_task(u - 1, UT - 1) + 1)
                    split_wo(step)
                if not first:
                    outputs_high(u)
                query_high(u, 1)
                act.wait_ge(k_loaded, u * 16 + 16)
                high(kT[:, 0], k_raw[:]).then_inc(k_high, 1)
                query_high(u, 2)
                act.wait_ge(v_loaded, u * 32 + 32)
                high(v_h[:], v_raw[:]).then_inc(v_high, 1)
                query_high(u, 3)
                for c in range(2):
                    act.wait_ge(scores_filled, u * 4 + 2 * c + 2)
                    blocks = slice(c * UB, (c + 1) * UB)
                    act.copy(s_lo[:, blocks, :], att_s[:, blocks, 1, :]).then_inc(s_lo_copied, 1)
                for c in range(2):
                    blocks = slice(c * UB, (c + 1) * UB)
                    act.wait_ge(shifted, u * 2 + c + 1)
                    nc.scalar.activation(s[:, blocks, :], s[:, blocks, :], ACT.Exp, scale=ATT_SCALE).then_inc(exp_done, 1)
                    if T == UNITS - 1:
                        split_w(step + 1, 2 * c)
                        split_w(step + 1, 2 * c + 1)

            for name in START:
                n = pos.get(name)
                if name[0] in "cx":
                    tile_high(name)
                elif name[0] == "bias":
                    for c in range(KC):
                        split_w(0, c)
                elif name[0] == "V" and name[2] == 2:
                    if name[1] > 0:
                        act.wait_ge(ring_filled, pos["K", name[1] - 1, 1, KVH - 1] + 1)
                    split_wo(name[1])
                elif name[0] == "K" and name[2:] == (0, 0):
                    act.wait_ge(ring_filled, n)
                    for c in range(KC):
                        split_w(name[1] + 1, c)
            unit(0, 0, True)
            for T in range(1, UNITS):
                unit(0, T, False)
            with act.Fori(1, NKV) as g:
                for T in range(UNITS):
                    unit(g, T, False)
            probs_high(NU)
            outputs_high(NU)
            for name in TAIL:
                n = pos.get(name)
                if name[0] == "f":
                    tile_high(name)
                elif name[0] == "A":
                    act.wait_ge(ring_filled, n + 1)
                    high(fw_h[:, :, 0:ER], ring[:, n % 2, :].rearrange("p (c n) -> p c n", c=KC)).then_inc(small_high, 1)
                elif name[0] == "router":
                    act.wait_ge(ring_filled, n + 1)
                    high(fw_h[:, :, ER:FN], ring[:, n % 2, 0:KC * E].rearrange("p (c n) -> p c n", c=KC)).then_inc(small_high, 1)
                elif name[0] == "Bm":
                    act.wait_ge(ring_filled, n + 1)
                    high(bm_h, ring[:, n % 2, :]).then_inc(small_high, 1)
                if name == ("f", TILES - 1) or name == ("e", ETILES - 1):
                    batch = 0 if name[0] == "f" else 1
                    act.wait_ge(gate_diff, batch + 1)
                    nc.scalar.activation(diff, diff, ACT.Exp).then_inc(gate_exp, 1)
                    for c in range(2):
                        act.wait_ge(hw_turned, batch * 2 + c + 1)
                        if batch > 0:
                            act.wait_ge(ring_filled, pos["e", batch * ETILES - 1] + 1)
                        high(hwT_h[:, c * 512:(c + 1) * 512], turn[:, c, :]).then_inc(hw_high, 1)

        @block.vector
        def _(dve):
            def low(dst, src, high_part):
                return nc.vector.tensor_tensor(dst, src, high_part.bitcast(F32), ALU.subtract)

            def tile_low(name):
                hi, lo = turned_tile(name)
                n = tile_no[name]
                dve.wait_ge(x_high, n + 1)
                low(lo, turn[:, n % 2, :].rearrange("p (c n) -> p c n", c=KC), hi).then_inc(tile_emptied, 1)

            def keys_or_values(name):
                m, n = kv_no[name], pos[name]
                if m >= SLOTS:
                    dve.wait_ge(kv_stored[m % SLOTS], kv_value[m - SLOTS])
                dve.wait_ge(ring_filled, n + 1)
                chunk = name[1] % CHUNKS
                if name[0] == "V":
                    ins = nc.vector.tensor_tensor(kv_stage[:, m % SLOTS, :], ring[:, n % 2, :],
                                                  bv_bc[:, chunk * D:(chunk + 1) * D], ALU.add)
                else:
                    head = NH + chunk * KVH + name[3]
                    ins = nc.vector.tensor_scalar(kv_stage[:, m % SLOTS, :], ring[:, n % 2, :], bias[:, head:head + 1],
                                                  None, ALU.add)
                ins.then_inc(ring_emptied, 1)

            def ln_stats(kind, t0):
                done = LN_STEPS * batches.index((kind, t0))
                four = slice(t0, t0 + 4)
                if kind == "f":
                    dve.wait_ge(ring_emptied, (pos["W", 3] if t0 == TILES - 4 else TAIL_TASKS - 1) + 1)
                for t in range(t0, t0 + 4):
                    if kind == "x":
                        dve.wait_ge(x_loaded[t], 16)
                    nc.vector.bn_stats(stats[:, t, :], y[:, t, :]).then_inc(ln_step, 1)
                dve.wait_ge(ln_step, done + 4)
                mean_e, mean_o = stats[:, four, 1], stats[:, four, 4]
                sq_e, sq_o = stats[:, four, 2], stats[:, four, 5]
                nc.vector.tensor_tensor(mean[:, four], mean_e, mean_o, ALU.add).then_inc(ln_step, 1)
                nc.vector.tensor_tensor(apart[:], mean_e, mean_o, ALU.subtract).then_inc(ln_step, 1)
                nc.vector.tensor_tensor(rstd[:, four], sq_e, sq_o, ALU.add).then_inc(ln_step, 1)
                dve.wait_ge(ln_step, done + 7)
                nc.vector.tensor_scalar(mean[:, four], mean[:, four], 0.5, None, ALU.mult).then_inc(ln_step, 1)
                nc.vector.tensor_tensor(apart[:], apart[:], apart[:], ALU.mult).then_inc(ln_step, 1)
                nc.vector.tensor_scalar(rstd[:, four], rstd[:, four], 1.0 / D, LN_EPS, ALU.mult,
                                        ALU.add).then_inc(ln_step, 1)
                dve.wait_ge(ln_step, done + 10)
                nc.vector.scalar_tensor_tensor(out=rstd[:, four], in0=apart[:], scalar=0.25, in1=rstd[:, four],
                                               op0=ALU.mult, op1=ALU.add).then_inc(var_ready, 1)

            def ln_tile(kind, t):
                n = norm_no[kind, t]
                if t % 4 == 0:
                    dve.wait_ge(rstd_ready, batches.index((kind, t)) + 1)
                if n >= 2:
                    dve.wait_ge(tile_filled, tile_no[norm_order[n - 2]] + 1)
                nc.vector.tensor_scalar(xn[:, n % 2, :], y[:, t, :], mean[:, t:t + 1], rstd[:, t:t + 1],
                                        ALU.subtract, ALU.mult).then_inc(xn_ready, 1)

            def s_max(u, c):
                blocks = slice(c * UB, (c + 1) * UB)
                dve.wait_ge(s_lo_copied, u * 2 + c + 1)
                nc.vector.tensor_tensor(s[:, blocks, :], att_s[:, blocks, 0, :], s_lo[:, blocks, :], ALU.add).then_inc(s_added, 1)
                dve.wait_ge(s_added, u * 2 + c + 1)
                nc.vector.tensor_reduce(row_max[:, blocks], s[:, blocks, :], AX, ALU.max).then_inc(max_done, 1)

            def s_sum(u, c):
                blocks = slice(c * UB, (c + 1) * UB)
                dve.wait_ge(exp_done, u * 2 + c + 1)
                nc.vector.tensor_reduce(row_sum[:, blocks], s[:, blocks, :], AX, ALU.add).then_inc(sum_done, 1)
                dve.wait_ge(sum_done, u * 2 + c + 1)
                nc.vector.reciprocal(row_inv[:, blocks], row_sum[:, blocks]).then_inc(inv_done, 1)

            def add_to_y(n, slot, t):
                dve.wait_ge(ring_filled, n + 1)
                nc.vector.tensor_tensor(y[:, t, :], ring[:, slot, :], y[:, t, :], ALU.add).then_inc(ring_emptied, 1)

            def query_low(u, h):
                dve.wait_ge(q_high, u * G + h + 1)
                nc.vector.scalar_tensor_tensor(
                    out=qT_l[:, :, h, :], in0=ring[:, q_slot(u, h), :].rearrange("p (b l) -> p b l", l=L),
                    scalar=g_bias[:, h:h + 1], in1=qT_h[:, :, h, :].bitcast(F32),
                    op0=ALU.add, op1=ALU.subtract).then_inc(ring_emptied, 1)

            def probs_low(u):
                for c in range(2):
                    dve.wait_ge(p_high, u * 2 - 1 + c)
                    t_c = turn[:, c, :].rearrange("p (b q) -> p b q", q=P)
                    b_c = slice(4 * c, 4 * c + 4)
                    low(pT[L:P, b_c, 0, :], t_c[0:L], pT[0:L, b_c, 0, :])
                    low(pT[0:L, b_c, 1, :], t_c[L:P], pT[L:P, b_c, 1, :]).then_inc(p_low, 1)

            def outputs_low(u):
                for j in range(4):
                    dve.wait_ge(o_high, u * 4 - 3 + j)
                    oh, ol = (o.rearrange("p h (n b l) -> p n b h l", b=2, l=L)[:, j] for o in (oT_h, oT_l))
                    low(ol, att_o[:, j], oh).then_inc(o_low, 1)

            def unit(g, T, first):
                u, T_prev = g * UNITS + T, (T + UNITS - 1) % UNITS

                def add_out(i):
                    if not first:
                        add_to_y(out_task(u, i), out_slot(i), T_prev * UT + i)

                if T == 0:
                    nc.vector.tensor_copy(g_bias[:], bias[:, bass.ds(g * G, G)]).then_inc(bias_ready, 1)
                    dve.wait_ge(bias_ready, g + 1)
                if not first:
                    probs_low(u)
                if isinstance(u, int) and u == 1:
                    dve.wait_ge(resid_ready, TILES)
                query_low(u, 0)
                if not first:
                    outputs_low(u)
                for h in range(1, G):
                    query_low(u, h)
                add_out(0)
                if first:
                    for m in range(len(kv_order) - SLOTS, len(kv_order)):
                        dve.wait_ge(kv_stored[m % SLOTS], kv_value[m])
                s_max(u, 0)
                s_max(u, 1)
                add_out(1)
                s_sum(u, 0)
                s_sum(u, 1)
                add_out(2)
                add_out(3)

            steps = count(1)

            def chain(ins):
                ins.then_inc(router_step, 1)
                dve.wait_ge(router_step, next(steps))

            def over(v):
                return v.unsqueeze(2).broadcast_to([P, ETILES, E])

            def first_max(values, peak, sel):
                chain(nc.vector.tensor_reduce(peak, values, AX, ALU.max))
                chain(nc.vector.tensor_tensor(mark, values, over(peak), ALU.is_ge))
                chain(nc.vector.tensor_tensor(mark, mark, rev[:].unsqueeze(1).broadcast_to([P, ETILES, E]), ALU.mult))
                chain(nc.vector.tensor_reduce(top, mark, AX, ALU.max))
                chain(nc.vector.tensor_tensor(sel, mark, over(top), ALU.is_equal))

            def router_choice(batch):
                dve.wait_ge(experts_filled, (batch + 1) * ETILES)
                chain(nc.vector.tensor_tensor(lg, att_f[:, :, ER:FN], rb_bc[:].unsqueeze(1).broadcast_to([P, ETILES, E]), ALU.add))
                first_max(lg, m1, sel1)
                chain(nc.vector.scalar_tensor_tensor(out=lg2, in0=sel1, scalar=SKIP, in1=lg, op0=ALU.mult, op1=ALU.add))
                first_max(lg2, m2, sel2)
                nc.vector.tensor_tensor(diff, m2, m1, ALU.subtract).then_inc(gate_diff, 1)

            def router_gates(batch):
                dve.wait_ge(gate_exp, batch + 1)
                chain(nc.vector.tensor_scalar(top, diff, 1.0, 1.0 / LORA_SCALE, ALU.add, ALU.mult))
                chain(nc.vector.reciprocal(gate1, top))
                chain(nc.vector.tensor_tensor(gate2, gate1, diff, ALU.mult))
                chain(nc.vector.tensor_tensor(sel1, sel1, over(gate1), ALU.mult))
                chain(nc.vector.tensor_tensor(sel2, sel2, over(gate2), ALU.mult))
                chain(nc.vector.tensor_tensor(sel1, sel1, sel2, ALU.add))
                for c in range(2):
                    if batch > 0:
                        dve.wait_ge(hw_turned, 2 * batch)
                    ts = slice(4 * c, 4 * c + 4)
                    nc.vector.tensor_tensor(hw[:, ts, :].rearrange("p t (e r) -> p t e r", e=E),
                                            att_f[:, ts, 0:ER].rearrange("p t (e r) -> p t e r", e=E),
                                            sel1[:, ts, :].unsqueeze(3).broadcast_to([P, 4, E, R]),
                                            ALU.mult).then_inc(hw_ready, 1)

            def hw_lows(batch):
                for c in range(2):
                    dve.wait_ge(hw_high, batch * 2 + c + 1)
                    low(hwT_l[:, c * 512:(c + 1) * 512], turn[:, c, :], hwT_h[:, c * 512:(c + 1) * 512]).then_inc(hw_low, 1)

            dve.wait_ge(const_ready, 2)
            for name in START_V:
                kind, n = name[0], pos.get(name)
                if kind == "bias":
                    dve.wait_ge(ring_filled, n + 1)
                    nc.vector.tensor_copy(bias[:], ring[:, n % 2, 0:NH + NKV]).then_inc(ring_emptied, 1)
                    dve.wait_ge(ring_emptied, n + 1)
                    dve.wait_ge(bias_loaded, 48)
                elif kind in "KV":
                    keys_or_values(name)
                elif kind == "S":
                    ln_stats(*name[1:])
                elif kind == "n":
                    ln_tile(*name[1:])
                else:
                    tile_low(name)
            dve.wait_ge(bc_loaded, 32)
            unit(0, 0, True)
            for T in range(1, UNITS):
                unit(0, T, False)
            with dve.Fori(1, NKV) as g:
                for T in range(UNITS):
                    unit(g, T, False)
            probs_low(NU)
            outputs_low(NU)
            for name in TAIL_V:
                kind, n = name[0], pos.get(name)
                if kind == "W":
                    add_to_y(n, n % 2, (UNITS - 1) * UT + name[1])
                elif kind == "S":
                    ln_stats(*name[1:])
                elif kind == "n":
                    ln_tile(*name[1:])
                elif kind == "f":
                    tile_low(name)
                elif kind == "A":
                    dve.wait_ge(small_high, 1)
                    low(fw_l[:, :, 0:ER], ring[:, n % 2, :].rearrange("p (c n) -> p c n", c=KC), fw_h[:, :, 0:ER]).then_inc(ring_emptied, 1)
                elif kind == "router":
                    dve.wait_ge(small_high, 2)
                    low(fw_l[:, :, ER:FN], ring[:, n % 2, 0:KC * E].rearrange("p (c n) -> p c n", c=KC), fw_h[:, :, ER:FN]).then_inc(ring_emptied, 1)
                elif kind == "Bm":
                    dve.wait_ge(small_high, 3)
                    low(bm_l, ring[:, n % 2, :], bm_h).then_inc(ring_emptied, 1)
                else:
                    add_to_y(n, n % 2, name[1])
                if name == ("f", TILES - 1) or name == ("e", ETILES - 1):
                    batch = 0 if kind == "f" else 1
                    router_choice(batch)
                    router_gates(batch)
                    hw_lows(batch)

        @block.tensor
        def _(pe):
            mm = nc.tensor.matmul

            def passes(dst, stat, mov, start, stop):
                mm(dst, stat[0], mov[0], start=start, stop=False)
                mm(dst, stat[0], mov[1], start=False, stop=False)
                return mm(dst, stat[1], mov[0], start=False, stop=stop)

            def wait_slot(n):
                if not isinstance(n, int) or n >= 2:
                    pe.wait_ge(ring_emptied, n - 1)

            def turn_columns(dst, src, width=P):
                rows = src.shape[0]
                for c in range(KC):
                    last = nc.tensor.transpose(dst[:, c * width:(c + 1) * width], src[:, c * P:(c + 1) * P],
                                               ident[0:rows, 0:rows])
                return last

            def turn_tile(name):
                (kind, t), n = name, tile_no[name]
                if kind == "c":
                    pe.wait_ge(c_loaded[t % PTILES], 16 * (t // PTILES + 1))
                    src = c_stage[:, t % PTILES, :]
                else:
                    pe.wait_ge(xn_ready, norm_no[name] + 1)
                    src = xn[:, norm_no[name] % 2, :]
                if n >= 2:
                    pe.wait_ge(tile_emptied, n - 1)
                if kind == "f" and t < 2:
                    pe.wait_ge(p_low, NU * 2)
                turn_columns(turn[:, n % 2, :], src).then_inc(tile_filled, 1)

            def values(name):
                _, step, t = name
                n = pos[name]
                tile = ("c", step // CHUNKS * PTILES + t)
                pe.wait_ge(tile_emptied, tile_no[tile] + 1)
                wait_slot(n)
                tokens_h, tokens_l = turned_tile(tile)
                for c in range(KC):
                    if t == 0:
                        pe.wait_ge(w_low, step * KC + c + 1)
                    last = passes(ring[:, n % 2, :], (tokens_h[:, c], tokens_l[:, c]), (w_h[:, c, :], w_l[:, c, :]),
                                  c == 0, c == KC - 1)
                last.then_inc(ring_filled, 1)

            def keys(name):
                _, step, b, k = name
                n, cols = pos[name], slice(k * HD, (k + 1) * HD)
                wait_slot(n)
                for c in range(KC):
                    if b == 0 and k == 0:
                        pe.wait_ge(wo_low, step * KC + c + 1)
                    last = passes(ring[:, n % 2, :], (wo_h[:, c, cols], wo_l[:, c, cols]),
                                  (cT[b][0][:, c, :], cT[b][1][:, c, :]), c == 0, c == KC - 1)
                last.then_inc(ring_filled, 1)

            def queries(g, T, u, h):
                tok, cols = slice(T * UTOK, (T + 1) * UTOK), slice(h * HD, (h + 1) * HD)
                wait_slot(q_task(u, h))
                for c in range(KC):
                    if T == 0 and h == 0:
                        pe.wait_ge(w_low, (STEPS + g) * KC + c + 1)
                    last = passes(ring[:, q_slot(u, h), :], (w_h[:, c, cols], w_l[:, c, cols]),
                                  (xT_h[:, c, tok], xT_l[:, c, tok]), c == 0, c == KC - 1)
                last.then_inc(ring_filled, 1)

            def out_project(u, n, slot, i):
                pe.wait_ge(o_low, u * 4 - 3 + i)
                wait_slot(n)
                tok = slice(i * P, (i + 1) * P)
                for h in range(G):
                    last = passes(ring[:, slot, :], (oT_h[:, h, tok], oT_l[:, h, tok]),
                                  (wo_h[:, h, :], wo_l[:, h, :]), h == 0, h == G - 1)
                last.then_inc(ring_filled, 1)

            def scores(u, first):
                pe.wait_ge(ring_emptied, q_task(u, G - 1) + 1)
                pe.wait_ge(k_low, u + 1)
                if not first:
                    pe.wait_ge(o_low, u * 4)
                for b in range(UB):
                    for hp in range(HP):
                        dst = att_s[:, b * HP + hp]
                        q_h, q_l = (q[:, b, 2 * hp:2 * hp + 2, :].rearrange("p h l -> p (h l)") for q in (qT_h, qT_l))
                        mm(dst, q_h, kT[:, :, b, :], start=True, stop=False)
                        last = mm(dst, q_l, kT[:, :, b, :], start=False, stop=True)
                    if b % 2:
                        last.then_inc(scores_filled, 1)

            def turn_probs(u, first):
                for c in range(2):
                    pe.wait_ge(probs_ready, u * 2 + c + 1)
                    if not first:
                        pe.wait_ge(p_low, u * 2)
                    for b in range(4 * c, 4 * c + 4):
                        last = nc.tensor.transpose(turn[:, c, (b % 4) * P:(b % 4 + 1) * P],
                                                   s[:, HP * b:HP * b + HP, :].rearrange("p k l -> p (k l)"), ident[:])
                    last.then_inc(p_turned, 1)

            def outputs(u):
                pe.wait_ge(v_low, u)
                for b in range(UB):
                    if b % 4 == 0:
                        pe.wait_ge(p_low, u * 2 - 1 + b // 4)
                    dst = att[:, b // 2, (b % 2) * 256:(b % 2 + 1) * 256]
                    probs = pT[:, b, :, :].rearrange("p k l -> p (k l)")
                    mm(dst, v_h[:, b, :], probs, start=True, stop=False)
                    last = mm(dst, v_l[:, b, :], probs, start=False, stop=True)
                    if b % 2:
                        last.then_inc(o_filled, 1)

            def unit(g, T, first):
                u = g * UNITS + T
                queries(g, T, u, 0)
                if not first:
                    outputs(u)
                for h in range(1, G):
                    queries(g, T, u, h)
                if T == 1:
                    pe.wait_ge(wo_low, (STEPS + g) * KC + KC)
                if not first:
                    out_project(u, out_task(u, 0), out_slot(0), 0)
                scores(u, first)
                if not first:
                    for i in range(1, UT):
                        out_project(u, out_task(u, i), out_slot(i), i)
                turn_probs(u, first)

            def down(t):
                batch, i = t // ETILES, t % ETILES
                if batch == 0:
                    pe.wait_ge(o_low, NU * 4)
                else:
                    pe.wait_ge(hw_ready, 2 * batch)
                pe.wait_ge(ring_emptied, pos["Bm",] + 1)
                pe.wait_ge(tile_emptied, tile_no["f", t] + 1)
                sl = slice(t * P, (t + 1) * P)
                for c in range(KC):
                    last = passes(att_f[:, i, 0:FN], (xT_h[:, c, sl], xT_l[:, c, sl]),
                                  (fw_h[:, c, :], fw_l[:, c, :]), c == 0, c == KC - 1)
                last.then_inc(experts_filled, 1)

            def turn_products(batch):
                for c in range(2):
                    pe.wait_ge(hw_ready, batch * 2 + c + 1)
                    if batch == 0:
                        pe.wait_ge(tile_emptied, tile_no["f", TILES - 1] + 1)
                    else:
                        pe.wait_ge(hw_low, batch * 2)
                    for t in range(4 * c, 4 * c + 4):
                        last = nc.tensor.transpose(turn[:, c, (t % 4) * P:(t % 4 + 1) * P], hw[:, t, :], ident[:])
                    last.then_inc(hw_turned, 1)

            def up(t):
                n, batch, i = pos["e", t], t // ETILES, t % ETILES
                pe.wait_ge(hw_low, batch * 2 + i // 4 + 1)
                wait_slot(n)
                sl = slice(i * P, (i + 1) * P)
                passes(ring[:, n % 2, :], (hwT_h[:, sl], hwT_l[:, sl]), (bm_h, bm_l),
                       True, True).then_inc(ring_filled, 1)

            pe.wait_ge(ident_ready, 1)
            for name in START:
                kind, n = name[0], pos.get(name)
                if kind == "bias":
                    rows = NH + NKV
                    wait_slot(n)
                    pe.wait_ge(bias_loaded, 48)
                    nc.tensor.transpose(ring[:, n % 2, 0:rows], bias_rows, ident[0:rows, 0:rows]).then_inc(ring_filled, 1)
                elif kind == "V":
                    values(name)
                elif kind == "K":
                    keys(name)
                else:
                    turn_tile(name)
            pe.wait_ge(tile_emptied, tile_no["x", TILES - 1] + 1)
            unit(0, 0, True)
            for T in range(1, UNITS):
                unit(0, T, False)
            with pe.Fori(1, NKV) as g:
                for T in range(UNITS):
                    unit(g, T, False)
            outputs(NU)
            for name in TAIL:
                kind, n = name[0], pos.get(name)
                i = name[1] if len(name) > 1 else None
                if kind == "W":
                    out_project(NU, n, n % 2, i)
                elif kind == "A":
                    pe.wait_ge(small_loaded, 16 * (2 + KC))
                    wait_slot(n)
                    turn_columns(ring[:, n % 2, :], a_rows).then_inc(ring_filled, 1)
                elif kind == "router":
                    wait_slot(n)
                    turn_columns(ring[:, n % 2, :], router_rows, E).then_inc(ring_filled, 1)
                elif kind == "Bm":
                    wait_slot(n)
                    turn_columns(ring[:, n % 2, :], bm_rows).then_inc(ring_filled, 1)
                elif kind == "f":
                    turn_tile(name)
                    if i >= 3 and i - 3 < ETILES:
                        down(i - 3)
                    if i == TILES - 1:
                        turn_products(0)
                else:
                    if i < ETILES:
                        down(ETILES + i)
                    if i == ETILES:
                        turn_products(1)
                    up(i)


_INS = ["x", "ctx_4096", "L0_xattn_Wq", "L0_xattn_bq", "L0_xattn_Wkv", "L0_xattn_bkv", "L0_xattn_Wo", "L0_xattn_bo",
        "L0_ffn_router_w", "L0_ffn_router_b", "L0_ffn_A", "L0_ffn_Bm"]


def kernel(**inputs):
    import numpy as _np
    import concourse.bacc as _bacc
    from concourse import mybir as _mybir
    from concourse.bass_utils import run_bass_kernel_spmd as _run

    nc = _bacc.Bacc("TRN2", target_bir_lowering=False, num_devices=1)
    arrays, args = {}, []
    for name in _INS:
        a = _np.ascontiguousarray(inputs[name])
        arrays[f"in_{name}_dram"] = a
        args.append(nc.dram_tensor(f"in_{name}_dram", a.shape, _mybir.dt.from_np(a.dtype), kind="ExternalInput").ap())
    args.append(nc.dram_tensor("out_dram", (B, L, D), F32, kind="ExternalOutput").ap())
    args.append(nc.dram_tensor("keys_dram", (NKV * HD, TOK), F32, kind="Internal").ap())
    args.append(nc.dram_tensor("values_dram", (NKV * L, B * HD), F32, kind="Internal").ap())
    build(nc, *args)
    r = _run(nc, [arrays], core_ids=[0])
    return r.results[0]["out_dram"]
```

```python
from contextlib import ExitStack
from itertools import count

import concourse.bass as bass
import concourse.mybir as mybir

F32 = mybir.dt.float32
F32R = mybir.dt.float32r
ACT = mybir.ActivationFunctionType
ALU = mybir.AluOpType
AX = mybir.AxisListType.X

P = 128
B, L, D = 32, 64, 512
NH, NKV, HD = 32, 8, 128
G = NH // NKV
KC = D // P
TOK = B * L
TILES = TOK // P
UTOK = 512
UNITS = TOK // UTOK
NU = NKV * UNITS
UB = UTOK // L
UT = UTOK // P
HP = G // 2
KVH = D // HD
CHUNKS = NKV // KVH
PARTS = 2
PTILES = TILES // PARTS
STEPS = PARTS * CHUNKS
E, R = 8, 16
ER = E * R
FN = ER + E
ETILES = 8
EBATCHES = TILES // ETILES
ATT_SCALE = 1.0 / float(HD) ** 0.5
LN_EPS = 1e-5
LORA_SCALE = 8.0 / R
SKIP = -3.0e38
SLOTS = 3
LN_STEPS = 10
UNIT_TASKS = G + UT


def parse(line):
    words = [(word, word.rstrip("0123456789")) for word in line.split()]
    return [(kind, int(word[len(kind):])) if len(word) > len(kind) else (kind,) for word, kind in words]


TENSOR_TAIL = parse(
    "A router f0 attend f1 Bm f2 W0 f3 W1 f4 W2 f5 W3 f6 down0 down1 f7 down2 f8 down3 f9 down4 f10 down5 f11 "
    "down6 f12 f13 down7 down8 down9 down10 products0 down11 down12 f14 f15 down13 e0 down14 e1 down15 e2 e3 e4 "
    "e5 products1 e6 e7 e8 e9 e10 e11 e12 e13 e14 e15")
VECTOR_TAIL = parse(
    "attend A router f0 norm2 outputs f1 norm3 Bm f2 norm4 W0 f3 norm5 W1 f4 norm6 W2 f5 norm7 W3 f6 norm8 "
    "stats12 f7 norm9 f8 norm10 f9 norm11 f10 norm12 f11 norm13 f12 norm14 f13 norm15 choice0 gates0 products0 "
    "f14 f15 e0 e1 choice1 e2 e3 gates1 e4 e5 products1 e6 e7 e8 e9 e10 e11 e12 e13 e14 e15")
SCALAR_TAIL = parse(
    "attend A router f0 outputs f1 Bm f2 f3 f4 f5 f6 f7 f8 f9 f10 f11 f12 f13 gates0 products0 f14 f15 gates1 "
    "products1")


def start_order():
    order = [("c", 0), ("c", 1), ("c", 2), ("c", 3)]
    for j in range(STEPS):
        part, chunk = j // CHUNKS, j % CHUNKS
        for t in range(PTILES):
            order.append(("V", j, t))
            if j == 0 and t == 0:
                order.append(("bias",))
            if chunk == 0 and t < 4:
                order.append(("c", part * PTILES + 4 + t))
            if t >= 4:
                order.append(("x", 4 * j + t - 4))
        for b in range(PTILES // 4):
            for k in range(KVH):
                order.append(("K", j, b, k))
                if b == 1 and chunk == CHUNKS - 1 and part + 1 < PARTS:
                    order.append(("c", (part + 1) * PTILES + k))
    return order


def start_vector_order(order):
    after = {}
    for j in range(STEPS):
        after["V", j, 1] = [("stats", 4 * j)]
        first = ("c", j // CHUNKS * PTILES + 7) if j % CHUNKS == 0 else ("V", j, 3)
        after[first] = [("norm", 4 * j), ("norm", 4 * j + 1)]
        after["x", 4 * j] = [("norm", 4 * j + 2)]
        after["x", 4 * j + 1] = [("norm", 4 * j + 3)]
    steps = []
    for name in order:
        steps += [name] + after.get(name, [])
    return steps


def build(nc, x, ctx_in, wq, bq, wkv, bkv, wo, bo, router_w, router_b, A, Bm, out, keys_dram, values_dram):
    ctx = ExitStack()
    with ctx:
        def sb(name, shape, dt=F32):
            return ctx.enter_context(nc.sbuf_tensor(name, shape, dt))

        def sem(name):
            return ctx.enter_context(nc.semaphore(name))

        x_rows = x.rearrange("b l d -> (b l) d")
        c_rows = ctx_in.rearrange("b l d -> (b l) d")
        out_rows = out.rearrange("b l d -> (b l) d")
        wq_v = wq.rearrange("(c p) n -> p c n", p=P)
        wkv_v = wkv.rearrange("(c p) n -> p c n", p=P)
        wo_v = wo.rearrange("(h p) n -> p h n", p=P)
        values_v = values_dram.rearrange("(g k) (b d) -> k g b d", k=L, d=HD)

        ident = sb("ident", [P, P])
        bias = sb("bias", [P, NH + NKV])
        g_bias = sb("g_bias", [P, G])
        rb_bc = sb("rb_bc", [P, E])
        rev = sb("rev", [P, E])
        y = sb("y", [P, TILES, D])
        c_stage, bias_rows = y[:, TILES - PTILES:TILES, :], y[0:NH + NKV, TILES - PTILES - 1, 0:HD]
        xT_h, xT_l = sb("xT_h", [P, KC, TOK], F32R), sb("xT_l", [P, KC, TOK], F32R)
        w_h, w_l = sb("w_h", [P, KC, D], F32R), sb("w_l", [P, KC, D], F32R)
        wo_h, wo_l = sb("wo_h", [P, G, D], F32R), sb("wo_l", [P, G, D], F32R)
        raw = sb("raw", [P, KC, D])
        a_rows, bm_rows, router_rows = raw[:, 0, :], raw[:, 1, :], raw[0:E, 2, :]
        qT_h, qT_l = sb("qT_h", [P, UB, G, L], F32R), sb("qT_l", [P, UB, G, L], F32R)
        oT_h, oT_l = sb("oT_h", [P, G, UTOK], F32R), sb("oT_l", [P, G, UTOK], F32R)
        cT = [tuple(q.rearrange("p b h l -> p (b h l)").rearrange("p (c n) -> p c n", c=KC) for q in (qT_h, qT_l)),
              (oT_h, oT_l)]
        (fw_h, bm_h), (fw_l, bm_l) = (
            (m[:, 0:KC * FN].rearrange("p (c n) -> p c n", c=KC), m[:, KC * FN:KC * FN + D])
            for m in (q.rearrange("p b h l -> p (b h l)") for q in (qT_h, qT_l)))
        k_raw = sb("k_raw", [P, UB, L])
        kT = sb("kT", [P, 2, UB, L], F32R)
        v_raw = sb("v_raw", [P, UB, HD])
        v_h, v_l = sb("v_h", [P, UB, HD], F32R), sb("v_l", [P, UB, HD], F32R)
        bv_bc, bo_bc = v_raw.rearrange("p b d -> p (b d)"), k_raw.rearrange("p b l -> p (b l)")
        s_mem = sb("s_mem", [P, SLOTS * D])
        kv_stage = s_mem.rearrange("p (t d) -> p t d", d=D)
        s = s_mem[:, 0:2 * D].rearrange("p (n l) -> p n l", l=L)
        hw = s_mem[:, 0:2 * D].rearrange("p (t n) -> p t n", n=ER)
        lg, lg2, sel1, sel2, mark = (
            s_mem[:, 2 * D + i * ETILES * E:2 * D + (i + 1) * ETILES * E].rearrange("p (t e) -> p t e", e=E)
            for i in range(5))
        m1, m2, top, diff, gate1, gate2 = (
            s_mem[:, 2 * D + 5 * ETILES * E + i * ETILES:2 * D + 5 * ETILES * E + (i + 1) * ETILES] for i in range(6))
        low_or_x = sb("low_or_x", [P, 2 * D])
        s_lo = low_or_x.rearrange("p (n l) -> p n l", l=L)
        xn = low_or_x.rearrange("p (t d) -> p t d", d=D)
        row_max = sb("row_max", [P, UB * HP])
        row_sum = sb("row_sum", [P, UB * HP])
        row_inv = sb("row_inv", [P, UB * HP])
        pT = sb("pT", [P, UB, HP, P], F32R)
        stats = sb("stats", [P, TILES, 6])
        mean, apart = sb("mean", [P, TILES]), sb("apart", [P, 4])
        rstd = sb("rstd", [P, TILES])
        exponent = sb("exponent", [P, 4])
        hwT_h, hwT_l = (o.rearrange("p h n -> p (h n)").rearrange("p (k n) -> p k n", k=EBATCHES) for o in (oT_h, oT_l))

        ring = ctx.enter_context(nc.psum_tensor("ring", [P, 2, 512], F32))
        att = ctx.enter_context(nc.psum_tensor("att", [P, 4, 512], F32))
        turn = ctx.enter_context(nc.psum_tensor("turn", [P, 2, 512], F32))
        att_s = att.rearrange("p n (b k l) -> p (n b) k l", k=2, l=L)
        att_o = att.rearrange("p n (b h l) -> p n b h l", b=2, h=G)
        att_f = att[:, :, 0:3 * FN].rearrange("p n (k f) -> p n k f", f=FN)

        bias_loaded, small_loaded, bc_loaded = sem("bias_loaded"), sem("small_loaded"), sem("bc_loaded")
        ident_cleared, ident_ready, const_ready = sem("ident_cleared"), sem("ident_ready"), sem("const_ready")
        w_loaded, wo_loaded, k_loaded, v_loaded = sem("w_loaded"), sem("wo_loaded"), sem("k_loaded"), sem("v_loaded")
        x_loaded = [sem(f"x_loaded{t}") for t in range(TILES)]
        c_loaded = [sem(f"c_loaded{t}") for t in range(PTILES)]
        kv_stored = [sem(f"kv_stored{t}") for t in range(SLOTS)]
        out_stored = sem("out_stored")
        ring_filled, tile_filled, scores_filled = sem("ring_filled"), sem("tile_filled"), sem("scores_filled")
        p_turned, o_filled = sem("p_turned"), sem("o_filled")
        experts_filled, hw_turned = sem("experts_filled"), sem("hw_turned")
        small_high, x_high, q_high, k_high = sem("small_high"), sem("x_high"), sem("q_high"), sem("k_high")
        s_lo_copied, exp_done = sem("s_lo_copied"), sem("exp_done")
        v_high, p_high, o_high = sem("v_high"), sem("p_high"), sem("o_high")
        w_high, wo_high = sem("w_high"), sem("wo_high")
        gate_exp, hw_high = sem("gate_exp"), sem("hw_high")
        ring_emptied, tile_emptied = sem("ring_emptied"), sem("tile_emptied")
        s_added, max_done = sem("s_added"), sem("max_done")
        sum_done, inv_done = sem("sum_done"), sem("inv_done")
        p_low, o_low, hw_low = sem("p_low"), sem("o_low"), sem("hw_low")
        ln_step, xn_ready, router_step, hw_ready = sem("ln_step"), sem("xn_ready"), sem("router_step"), sem("hw_ready")
        bias_ready, gate_diff, var_ready = sem("bias_ready"), sem("gate_diff"), sem("var_ready")
        shifted, probs_ready, w_low, wo_low = sem("shifted"), sem("probs_ready"), sem("w_low"), sem("wo_low")
        k_low, v_low, resid_ready, rstd_ready = sem("k_low"), sem("v_low"), sem("resid_ready"), sem("rstd_ready")

        START = start_order()
        ring_start = [name for name in START if name[0] not in ("c", "x")]
        ring_tail = [name for name in TENSOR_TAIL if name[0] in ("A", "router", "Bm", "W", "e")]
        pos = {name: n for n, name in enumerate(ring_start)}
        FIRST_UNIT = len(ring_start)
        TAIL_TASKS = FIRST_UNIT + G + UNIT_TASKS * (NU - 1)
        pos.update({name: TAIL_TASKS + n for n, name in enumerate(ring_tail)})

        def q_task(u, h):
            return FIRST_UNIT + h if isinstance(u, int) and u == 0 else FIRST_UNIT + G + UNIT_TASKS * (u - 1) + h

        def out_task(u, i):
            return FIRST_UNIT + G + UNIT_TASKS * (u - 1) + G + i

        def q_slot(u, h):
            return (FIRST_UNIT + h) % 2

        def out_slot(i):
            return out_task(1, i) % 2

        tile_no = {name: n for n, name in enumerate(name for name in START + TENSOR_TAIL if name[0] in ("c", "x", "f"))}
        norm_order = [name for name in START + TENSOR_TAIL if name[0] in ("x", "f")]
        norm_no = {name: n for n, name in enumerate(norm_order)}
        batches = [("x", t) for t in range(0, TILES, 4)] + [("f", t) for t in range(0, TILES, 4)]
        kv_order = [name for name in START if name[0] in ("K", "V")]
        kv_no = {name: m for m, name in enumerate(kv_order)}
        kv_value = []
        for m, name in enumerate(kv_order):
            kv_value.append((kv_value[m - SLOTS] if m >= SLOTS else 0) + (32 if name[0] == "V" else 16))

        def turned_tile(name):
            kind, t = name
            if kind != "c":
                return xT_h[:, :, t * P:(t + 1) * P], xT_l[:, :, t * P:(t + 1) * P]
            return tuple(part[:, :, (t % 4) * P:(t % 4 + 1) * P] for part in cT[t % PTILES // 4])

        EXPERT_BANKS = ((0, 1, 2), (3, 0, 1))

        def expert_place(t):
            batch, i = t // ETILES, t % ETILES
            return EXPERT_BANKS[batch][i // 3], i % 3

        def expert_banks(batch):
            return [(bank, slice(3 * n, min(3 * n + 3, ETILES))) for n, bank in enumerate(EXPERT_BANKS[batch])]

        block = ctx.enter_context(nc.Block())

        @block.sync
        def _(sp):
            def load_w(step, src, col):
                if not isinstance(step, int) or step > 0:
                    sp.wait_ge(wo_low, step * KC)
                sp.dma_start(raw[:], src[:, :, bass.ds(col, D)]).then_inc(w_loaded, 16)

            def load_wo(step, src):
                sp.wait_ge(w_low, step * KC + KC)
                sp.dma_start(raw[:], src).then_inc(wo_loaded, 16)

            def load_c(t):
                if t >= PTILES:
                    sp.wait_ge(tile_filled, tile_no["c", t - PTILES] + 1)
                sp.dma_start(c_stage[:, t % PTILES, :], c_rows[t * P:(t + 1) * P, :]).then_inc(c_loaded[t % PTILES], 16)

            def load_x(t):
                sp.dma_start(y[:, t, :], x_rows[t * P:(t + 1) * P, :]).then_inc(x_loaded[t], 16)

            def store_kv(name):
                m = kv_no[name]
                sp.wait_ge(ring_emptied, pos[name] + 1)
                part, chunk = name[1] // CHUNKS, name[1] % CHUNKS
                if name[0] == "V":
                    for i in range(2):
                        sp.dma_start(values_v[:, chunk * KVH:(chunk + 1) * KVH, 2 * (part * PTILES + name[2]) + i, :],
                                     kv_stage[i * L:(i + 1) * L, m % SLOTS, :].rearrange("p (g d) -> p g d", d=HD)
                                     ).then_inc(kv_stored[m % SLOTS], 16)
                else:
                    r0, c0 = (chunk * KVH + name[3]) * HD, (part * (PTILES // 4) + name[2]) * UTOK
                    sp.dma_start(keys_dram[r0:r0 + HD, c0:c0 + UTOK], kv_stage[:, m % SLOTS, :]).then_inc(kv_stored[m % SLOTS], 16)

            def values_weights(step):
                load_w(step, wkv_v, NKV * HD + step % CHUNKS * D)

            for t in range(4):
                load_c(t)
            values_weights(0)
            sp.dma_start(bias_rows[0:NH, :], bq.rearrange("(h p) -> h p", p=HD)).then_inc(bias_loaded, 16)
            sp.dma_start(bias_rows[NH:NH + NKV, :], bkv[0:NKV * HD].rearrange("(h p) -> h p", p=HD)).then_inc(bias_loaded, 16)
            sp.dma_start(bv_bc, bkv[NKV * HD:2 * NKV * HD].rearrange("(a d) -> a d", a=1).broadcast_to([P, NKV * HD])
                         ).then_inc(bias_loaded, 16)
            for t in range(4, 8):
                load_c(t)
            for t in range(4):
                load_x(t)
            sp.dma_start(bo_bc, bo.rearrange("(a d) -> a d", a=1).broadcast_to([P, D])).then_inc(bc_loaded, 16)
            sp.dma_start(rb_bc[:], router_b.rearrange("(a d) -> a d", a=1).broadcast_to([P, E])).then_inc(bc_loaded, 16)
            for name in START:
                if name[0] in ("K", "V"):
                    if name[0] == "V" and name[2] == 0:
                        load_wo(name[1], wkv_v[:, :, name[1] % CHUNKS * D:(name[1] % CHUNKS + 1) * D])
                    if name == ("V", 0, 0):
                        sp.wait_ge(ring_filled, pos["bias",] + 1)
                        for t in range(4, TILES - PTILES):
                            load_x(t)
                    store_kv(name)
                    if name[0] == "K" and name[2:] == (0, 1):
                        if name[1] + 1 < STEPS:
                            values_weights(name[1] + 1)
                        else:
                            load_w(STEPS, wq_v, 0)
                if name[0] == "c" and 4 <= name[1] < PTILES:
                    load_c(name[1] + 4)
                    if name[1] == PTILES - 1:
                        for t in range(PTILES + 4, TILES):
                            load_c(t)
                if name in (("K", 1, 1, 3), ("V", 2, 4)):
                    last = 11 if name[0] == "K" else 15
                    sp.wait_ge(tile_filled, tile_no["c", last] + 1)
                    for t in range(last - 3, last + 1):
                        load_x(t)

            def unit(g, T, first):
                step, u = STEPS + g, g * UNITS + T
                if first:
                    sp.wait_ge(resid_ready, TILES)
                    m = kv_no["K", 0, 0, 0]
                    sp.wait_ge(kv_stored[m % SLOTS], kv_value[m])
                else:
                    if isinstance(u, int) and u == 1:
                        for m in range(len(kv_order) - SLOTS, len(kv_order)):
                            sp.wait_ge(kv_stored[m % SLOTS], kv_value[m])
                    sp.wait_ge(scores_filled, u * UB // 2)
                sp.dma_start(k_raw.rearrange("p b l -> p (b l)"),
                             keys_dram[bass.ds(g * HD, HD), T * UTOK:(T + 1) * UTOK]).then_inc(k_loaded, 16)
                if T == 0:
                    load_wo(step, wo_v[:, bass.ds(g * G, G), :])
                if T == 2 and isinstance(g, int) and g == NKV - 1:
                    sp.wait_ge(wo_low, step * KC + KC)
                    sp.dma_start(a_rows, A.rearrange("e r d -> (e r) d")).then_inc(small_loaded, 16)
                    sp.dma_start(router_rows, router_w).then_inc(small_loaded, 16)
                    for c in range(KC):
                        sp.dma_start(bm_rows.rearrange("p (c e r) -> p c e r", c=KC, e=E)[:, c],
                                     Bm[:, c * P:(c + 1) * P, :].rearrange("e p r -> p e r")).then_inc(small_loaded, 16)
                elif T == 2:
                    load_w(step + 1, wq_v, (g + 1) * (G * HD))
                if first:
                    sp.wait_ge(ring_emptied, pos["V", STEPS - 1, PTILES - 1] + 1)
                    for m in range(SLOTS):
                        m += kv_no["V", 0, 3]
                        sp.wait_ge(kv_stored[m % SLOTS], kv_value[m])
                else:
                    sp.wait_ge(o_filled, u * UB // 2)
                for i in range(2):
                    sp.dma_start(v_raw[i * L:(i + 1) * L].rearrange("p b d -> p (b d)"),
                                 values_dram[bass.ds(g * L, L), T * UB * HD:(T + 1) * UB * HD]).then_inc(v_loaded, 16)

            unit(0, 0, True)
            for T in range(1, UNITS):
                unit(0, T, False)
            with sp.Fori(1, NKV - 1) as g:
                for T in range(UNITS):
                    unit(g, T, False)
            for T in range(UNITS):
                unit(NKV - 1, T, False)
            for t in range(TILES):
                sp.wait_ge(ring_emptied, pos["e", t] + 1)
                sp.dma_start(out_rows[t * P:(t + 1) * P, :], y[:, t, :]).then_inc(out_stored, 16)
            sp.wait_ge(out_stored, 16 * TILES)

        @block.gpsimd
        def _(pool):
            nc.gpsimd.memset(ident[:], 0.0).then_inc(ident_cleared, 1)
            pool.wait_ge(ident_cleared, 1)
            nc.gpsimd.affine_select(out=ident[:], in_=ident[:], compare_op=ALU.not_equal, fill=1.0, base=0,
                                    pattern=[[-1, P]], channel_multiplier=1).then_inc(ident_ready, 1)
            nc.gpsimd.memset(exponent[:], -0.5).then_inc(const_ready, 1)
            for e in range(E):
                last = nc.gpsimd.memset(rev[:, e:e + 1], float(E - e))
            last.then_inc(const_ready, 1)
            pool.wait_ge(const_ready, 2)

            def low(dst, src, high_part):
                return nc.gpsimd.tensor_tensor(dst, src, high_part.bitcast(F32), ALU.subtract)

            def split_w(step, c):
                pool.wait_ge(w_high, step * KC + c + 1)
                low(w_l[:, c, :], raw[:, c, :], w_h[:, c, :]).then_inc(w_low, 1)

            def split_wo(step):
                for c in range(KC):
                    pool.wait_ge(wo_high, step * KC + c + 1)
                    low(wo_l[:, c, :], raw[:, c, :], wo_h[:, c, :]).then_inc(wo_low, 1)

            def shift(u, c):
                blocks = slice(c * UB, (c + 1) * UB)
                pool.wait_ge(max_done, u * 2 + c + 1)
                nc.gpsimd.tensor_tensor(s[:, blocks, :], s[:, blocks, :],
                                        row_max[:, blocks].unsqueeze(2).broadcast_to([P, UB, L]),
                                        ALU.subtract).then_inc(shifted, 1)

            def normalise(u, c):
                blocks = slice(c * UB, (c + 1) * UB)
                pool.wait_ge(inv_done, u * 2 + c + 1)
                nc.gpsimd.tensor_tensor(s[:, blocks, :], s[:, blocks, :],
                                        row_inv[:, blocks].unsqueeze(2).broadcast_to([P, UB, L]),
                                        ALU.mult).then_inc(probs_ready, 1)

            def root(kind, t0):
                pool.wait_ge(var_ready, batches.index((kind, t0)) + 1)
                nc.gpsimd.tensor_tensor(rstd[:, t0:t0 + 4], rstd[:, t0:t0 + 4], exponent[:],
                                        ALU.pow).then_inc(rstd_ready, 1)

            def unit(g, T, first):
                step, u = STEPS + g, g * UNITS + T
                last_group = isinstance(g, int) and g == NKV - 1
                if T == 1:
                    split_wo(step)
                pool.wait_ge(k_high, u + 1)
                low(kT[:, 1], k_raw[:], kT[:, 0]).then_inc(k_low, 1)
                pool.wait_ge(v_high, u + 1)
                low(v_l[:], v_raw[:], v_h[:]).then_inc(v_low, 1)
                if last_group and T >= 2:
                    root("f", 4 * (T - 2))
                shift(u, 0)
                shift(u, 1)
                if T == UNITS - 1 and not last_group:
                    split_w(step + 1, 0)
                normalise(u, 0)
                normalise(u, 1)
                if T == UNITS - 1 and not last_group:
                    for c in range(1, KC):
                        split_w(step + 1, c)

            for j in range(STEPS):
                root("x", 4 * j)
                split_wo(j)
                if j == 0:
                    pool.wait_ge(bc_loaded, 32)
                for t in range(4 * j, 4 * j + 4):
                    pool.wait_ge(xn_ready, norm_no["x", t] + 1)
                    nc.gpsimd.tensor_tensor(y[:, t, :], y[:, t, :], bo_bc, ALU.add).then_inc(resid_ready, 1)
                for c in range(KC):
                    split_w(j + 1, c)
            unit(0, 0, True)
            for T in range(1, UNITS):
                unit(0, T, False)
            with pool.Fori(1, NKV - 1) as g:
                for T in range(UNITS):
                    unit(g, T, False)
            for T in range(UNITS):
                unit(NKV - 1, T, False)
            root("f", TILES - 8)
            root("f", TILES - 4)

        @block.scalar
        def _(act):
            def high(dst, src, bias_ap=None):
                if bias_ap is None:
                    return nc.scalar.activation(dst, src, ACT.Copy)
                return nc.scalar.activation(dst, src, ACT.Identity, bias=bias_ap)

            def split_w(step, c):
                if c == 0:
                    act.wait_ge(w_loaded, step * 16 + 16)
                high(w_h[:, c, :], raw[:, c, :]).then_inc(w_high, 1)

            def split_wo(step):
                act.wait_ge(wo_loaded, step * 16 + 16)
                for c in range(KC):
                    high(wo_h[:, c, :], raw[:, c, :]).then_inc(wo_high, 1)

            def tile_high(name):
                n = tile_no[name]
                act.wait_ge(tile_filled, n + 1)
                high(turned_tile(name)[0], turn[:, n % 2, :].rearrange("p (c n) -> p c n", c=KC)).then_inc(x_high, 1)

            def query_high(u, h):
                act.wait_ge(ring_filled, q_task(u, h) + 1)
                high(qT_h[:, :, h, :], ring[:, q_slot(u, h), :].rearrange("p (b l) -> p b l", l=L),
                     g_bias[:, h:h + 1]).then_inc(q_high, 1)

            def probs_high(u):
                for c in range(2):
                    act.wait_ge(p_turned, u * 2 - 1 + c)
                    t_c = turn[:, c, :].rearrange("p (b q) -> p b q", q=P)
                    high(pT[0:L, 4 * c:4 * c + 4, 0, :], t_c[0:L])
                    high(pT[L:P, 4 * c:4 * c + 4, 1, :], t_c[L:P]).then_inc(p_high, 1)

            def outputs_high(u):
                for j in range(4):
                    act.wait_ge(o_filled, u * 4 - 3 + j)
                    high(oT_h.rearrange("p h (n b l) -> p n b h l", b=2, l=L)[:, j], att_o[:, j]).then_inc(o_high, 1)

            def unit(g, T, first):
                step, u = STEPS + g, g * UNITS + T
                last_group = isinstance(g, int) and g == NKV - 1
                second = isinstance(u, int) and u == 1
                if not first and not second:
                    probs_high(u)
                if T == 0:
                    act.wait_ge(bias_ready, g + 1)
                query_high(u, 0)
                if T == 1:
                    if not second:
                        act.wait_ge(ring_filled, out_task(u - 1, UT - 1) + 1)
                    split_wo(step)
                if second:
                    probs_high(u)
                    query_high(u, 1)
                if not first:
                    outputs_high(u)
                if not second:
                    query_high(u, 1)
                act.wait_ge(k_loaded, u * 16 + 16)
                high(kT[:, 0], k_raw[:]).then_inc(k_high, 1)
                query_high(u, 2)
                act.wait_ge(v_loaded, u * 32 + 32)
                high(v_h[:], v_raw[:]).then_inc(v_high, 1)
                query_high(u, 3)
                for c in range(2):
                    act.wait_ge(scores_filled, u * 4 + 2 * c + 2)
                    blocks = slice(c * UB, (c + 1) * UB)
                    act.copy(s_lo[:, blocks, :], att_s[:, blocks, 1, :]).then_inc(s_lo_copied, 1)
                for c in range(2):
                    blocks = slice(c * UB, (c + 1) * UB)
                    act.wait_ge(shifted, u * 2 + c + 1)
                    nc.scalar.activation(s[:, blocks, :], s[:, blocks, :], ACT.Exp, scale=ATT_SCALE).then_inc(exp_done, 1)
                    if T == UNITS - 1 and not last_group:
                        split_w(step + 1, 2 * c)
                        split_w(step + 1, 2 * c + 1)

            for name in START:
                n = pos.get(name)
                if name[0] in ("c", "x"):
                    tile_high(name)
                elif name[0] == "bias":
                    for c in range(KC):
                        split_w(0, c)
                elif name[0] == "V" and name[2] == 2:
                    if name[1] > 0:
                        act.wait_ge(ring_filled, pos["K", name[1] - 1, 1, KVH - 1] + 1)
                    split_wo(name[1])
                elif name[0] == "K" and name[2:] == (0, 0):
                    act.wait_ge(ring_filled, n)
                    for c in range(KC):
                        split_w(name[1] + 1, c)
            unit(0, 0, True)
            for T in range(1, UNITS):
                unit(0, T, False)
            with act.Fori(1, NKV - 1) as g:
                for T in range(UNITS):
                    unit(g, T, False)
            for T in range(UNITS):
                unit(NKV - 1, T, False)
            for name in SCALAR_TAIL:
                kind, n = name[0], pos.get(name)
                if kind == "attend":
                    probs_high(NU)
                elif kind == "outputs":
                    outputs_high(NU)
                elif kind == "f":
                    tile_high(name)
                elif kind == "A":
                    act.wait_ge(ring_filled, n + 1)
                    high(fw_h[:, :, 0:ER], ring[:, n % 2, :].rearrange("p (c n) -> p c n", c=KC)).then_inc(small_high, 1)
                elif kind == "router":
                    act.wait_ge(ring_filled, n + 1)
                    high(fw_h[:, :, ER:FN], ring[:, n % 2, 0:KC * E].rearrange("p (c n) -> p c n", c=KC)).then_inc(small_high, 1)
                elif kind == "Bm":
                    act.wait_ge(ring_filled, n + 1)
                    high(bm_h, ring[:, n % 2, :]).then_inc(small_high, 1)
                elif kind == "gates":
                    act.wait_ge(gate_diff, name[1] + 1)
                    nc.scalar.activation(diff, diff, ACT.Exp).then_inc(gate_exp, 1)
                else:
                    for c in range(2):
                        act.wait_ge(hw_turned, name[1] * 2 + c + 1)
                        high(hwT_h[:, name[1], c * 512:(c + 1) * 512], turn[:, c, :]).then_inc(hw_high, 1)

        @block.vector
        def _(dve):
            def low(dst, src, high_part):
                return nc.vector.tensor_tensor(dst, src, high_part.bitcast(F32), ALU.subtract)

            def tile_low(name):
                hi, lo = turned_tile(name)
                n = tile_no[name]
                dve.wait_ge(x_high, n + 1)
                low(lo, turn[:, n % 2, :].rearrange("p (c n) -> p c n", c=KC), hi).then_inc(tile_emptied, 1)

            def keys_or_values(name):
                m, n = kv_no[name], pos[name]
                if m == 0:
                    dve.wait_ge(bias_loaded, 48)
                if m >= SLOTS:
                    dve.wait_ge(kv_stored[m % SLOTS], kv_value[m - SLOTS])
                dve.wait_ge(ring_filled, n + 1)
                chunk = name[1] % CHUNKS
                if name[0] == "V":
                    ins = nc.vector.tensor_tensor(kv_stage[:, m % SLOTS, :], ring[:, n % 2, :],
                                                  bv_bc[:, chunk * D:(chunk + 1) * D], ALU.add)
                else:
                    head = NH + chunk * KVH + name[3]
                    ins = nc.vector.tensor_scalar(kv_stage[:, m % SLOTS, :], ring[:, n % 2, :], bias[:, head:head + 1],
                                                  None, ALU.add)
                ins.then_inc(ring_emptied, 1)

            def ln_stats(kind, t0):
                for t in range(t0, t0 + 4):
                    tile_stats(kind, t)
                ln_combine(kind, t0)

            def tile_stats(kind, t):
                t0 = t // 4 * 4
                if kind == "f":
                    last = pos["W", 3] if t0 == TILES - 4 else out_task((NKV - 1) * UNITS + t0 // UT + 1, UT - 1)
                    dve.wait_ge(ring_emptied, last - 3 + t % 4 + 1)
                else:
                    dve.wait_ge(x_loaded[t], 16)
                nc.vector.bn_stats(stats[:, t, :], y[:, t, :]).then_inc(ln_step, 1)

            def ln_combine(kind, t0):
                done, four = LN_STEPS * batches.index((kind, t0)), slice(t0, t0 + 4)
                dve.wait_ge(ln_step, done + 4)
                mean_e, mean_o = stats[:, four, 1], stats[:, four, 4]
                sq_e, sq_o = stats[:, four, 2], stats[:, four, 5]
                nc.vector.tensor_tensor(mean[:, four], mean_e, mean_o, ALU.add).then_inc(ln_step, 1)
                nc.vector.tensor_tensor(apart[:], mean_e, mean_o, ALU.subtract).then_inc(ln_step, 1)
                nc.vector.tensor_tensor(rstd[:, four], sq_e, sq_o, ALU.add).then_inc(ln_step, 1)
                dve.wait_ge(ln_step, done + 7)
                nc.vector.tensor_scalar(mean[:, four], mean[:, four], 0.5, None, ALU.mult).then_inc(ln_step, 1)
                nc.vector.tensor_tensor(apart[:], apart[:], apart[:], ALU.mult).then_inc(ln_step, 1)
                nc.vector.tensor_scalar(rstd[:, four], rstd[:, four], 1.0 / D, LN_EPS, ALU.mult,
                                        ALU.add).then_inc(ln_step, 1)
                dve.wait_ge(ln_step, done + 10)
                nc.vector.scalar_tensor_tensor(out=rstd[:, four], in0=apart[:], scalar=0.25, in1=rstd[:, four],
                                               op0=ALU.mult, op1=ALU.add).then_inc(var_ready, 1)

            def ln_tile(kind, t):
                n = norm_no[kind, t]
                if t % 4 == 0:
                    dve.wait_ge(rstd_ready, batches.index((kind, t)) + 1)
                if n >= 2:
                    dve.wait_ge(tile_filled, tile_no[norm_order[n - 2]] + 1)
                nc.vector.tensor_scalar(xn[:, n % 2, :], y[:, t, :], mean[:, t:t + 1], rstd[:, t:t + 1],
                                        ALU.subtract, ALU.mult).then_inc(xn_ready, 1)

            def s_max(u, c):
                blocks = slice(c * UB, (c + 1) * UB)
                dve.wait_ge(s_lo_copied, u * 2 + c + 1)
                nc.vector.tensor_tensor(s[:, blocks, :], att_s[:, blocks, 0, :], s_lo[:, blocks, :], ALU.add).then_inc(s_added, 1)
                dve.wait_ge(s_added, u * 2 + c + 1)
                nc.vector.tensor_reduce(row_max[:, blocks], s[:, blocks, :], AX, ALU.max).then_inc(max_done, 1)

            def s_sum(u, c):
                blocks = slice(c * UB, (c + 1) * UB)
                dve.wait_ge(exp_done, u * 2 + c + 1)
                nc.vector.tensor_reduce(row_sum[:, blocks], s[:, blocks, :], AX, ALU.add).then_inc(sum_done, 1)
                dve.wait_ge(sum_done, u * 2 + c + 1)
                nc.vector.reciprocal(row_inv[:, blocks], row_sum[:, blocks]).then_inc(inv_done, 1)

            def add_to_y(n, slot, t):
                dve.wait_ge(ring_filled, n + 1)
                nc.vector.tensor_tensor(y[:, t, :], ring[:, slot, :], y[:, t, :], ALU.add).then_inc(ring_emptied, 1)

            def query_low(u, h):
                dve.wait_ge(q_high, u * G + h + 1)
                nc.vector.scalar_tensor_tensor(
                    out=qT_l[:, :, h, :], in0=ring[:, q_slot(u, h), :].rearrange("p (b l) -> p b l", l=L),
                    scalar=g_bias[:, h:h + 1], in1=qT_h[:, :, h, :].bitcast(F32),
                    op0=ALU.add, op1=ALU.subtract).then_inc(ring_emptied, 1)

            def probs_low(u):
                for c in range(2):
                    dve.wait_ge(p_high, u * 2 - 1 + c)
                    t_c = turn[:, c, :].rearrange("p (b q) -> p b q", q=P)
                    b_c = slice(4 * c, 4 * c + 4)
                    low(pT[L:P, b_c, 0, :], t_c[0:L], pT[0:L, b_c, 0, :])
                    low(pT[0:L, b_c, 1, :], t_c[L:P], pT[L:P, b_c, 1, :]).then_inc(p_low, 1)

            def outputs_low(u):
                for j in range(4):
                    dve.wait_ge(o_high, u * 4 - 3 + j)
                    oh, ol = (o.rearrange("p h (n b l) -> p n b h l", b=2, l=L)[:, j] for o in (oT_h, oT_l))
                    low(ol, att_o[:, j], oh).then_inc(o_low, 1)

            def unit(g, T, first):
                u, T_prev = g * UNITS + T, (T + UNITS - 1) % UNITS

                def add_out(i):
                    if not first:
                        add_to_y(out_task(u, i), out_slot(i), T_prev * UT + i)

                if T == 0:
                    nc.vector.tensor_copy(g_bias[:], bias[:, bass.ds(g * G, G)]).then_inc(bias_ready, 1)
                    dve.wait_ge(bias_ready, g + 1)
                second = isinstance(u, int) and u == 1
                if not first and not second:
                    probs_low(u)
                query_low(u, 0)
                if second:
                    dve.wait_ge(resid_ready, TILES)
                    probs_low(u)
                    query_low(u, 1)
                if not first:
                    outputs_low(u)
                if not second:
                    query_low(u, 1)
                for h in range(2, G):
                    query_low(u, h)
                if isinstance(g, int) and g == NKV - 1 and T >= 2:
                    ln_stats("f", 4 * (T - 2))
                add_out(0)
                if first:
                    for m in range(len(kv_order) - SLOTS, len(kv_order)):
                        dve.wait_ge(kv_stored[m % SLOTS], kv_value[m])
                s_max(u, 0)
                s_max(u, 1)
                last = isinstance(u, int) and u == NU - 1
                if last:
                    ln_tile("f", 0)
                    ln_tile("f", 1)
                add_out(1)
                s_sum(u, 0)
                s_sum(u, 1)
                add_out(2)
                if last:
                    for t in range(TILES - 2 * UT, TILES - UT - 1):
                        tile_stats("f", t)
                add_out(3)
                if last:
                    tile_stats("f", TILES - UT - 1)
                    ln_combine("f", TILES - 2 * UT)

            steps = count(1)

            def chain(ins):
                ins.then_inc(router_step, 1)
                dve.wait_ge(router_step, next(steps))

            def over(v):
                return v.unsqueeze(2).broadcast_to([P, ETILES, E])

            def first_max(values, peak, sel):
                chain(nc.vector.tensor_reduce(peak, values, AX, ALU.max))
                chain(nc.vector.tensor_tensor(mark, values, over(peak), ALU.is_ge))
                chain(nc.vector.tensor_tensor(mark, mark, rev[:].unsqueeze(1).broadcast_to([P, ETILES, E]), ALU.mult))
                chain(nc.vector.tensor_reduce(top, mark, AX, ALU.max))
                chain(nc.vector.tensor_tensor(sel, mark, over(top), ALU.is_equal))

            def router_choice(batch):
                dve.wait_ge(experts_filled, (batch + 1) * ETILES)
                for bank, ts in expert_banks(batch):
                    n = ts.stop - ts.start
                    last = nc.vector.tensor_tensor(lg[:, ts, :], att_f[:, bank, 0:n, ER:FN],
                                                   rb_bc[:].unsqueeze(1).broadcast_to([P, n, E]), ALU.add)
                chain(last)
                first_max(lg, m1, sel1)
                chain(nc.vector.scalar_tensor_tensor(out=lg2, in0=sel1, scalar=SKIP, in1=lg, op0=ALU.mult, op1=ALU.add))
                first_max(lg2, m2, sel2)
                nc.vector.tensor_tensor(diff, m2, m1, ALU.subtract).then_inc(gate_diff, 1)

            def router_gates(batch):
                dve.wait_ge(gate_exp, batch + 1)
                chain(nc.vector.tensor_scalar(top, diff, 1.0, 1.0 / LORA_SCALE, ALU.add, ALU.mult))
                chain(nc.vector.reciprocal(gate1, top))
                chain(nc.vector.tensor_tensor(gate2, gate1, diff, ALU.mult))
                chain(nc.vector.tensor_tensor(sel1, sel1, over(gate1), ALU.mult))
                chain(nc.vector.tensor_tensor(sel2, sel2, over(gate2), ALU.mult))
                chain(nc.vector.tensor_tensor(sel1, sel1, sel2, ALU.add))
                if batch > 0:
                    dve.wait_ge(hw_turned, 2 * batch)
                for bank, ts in expert_banks(batch):
                    n = ts.stop - ts.start
                    nc.vector.tensor_tensor(hw[:, ts, :].rearrange("p t (e r) -> p t e r", e=E),
                                            att_f[:, bank, 0:n, 0:ER].rearrange("p t (e r) -> p t e r", e=E),
                                            sel1[:, ts, :].unsqueeze(3).broadcast_to([P, n, E, R]),
                                            ALU.mult).then_inc(hw_ready, 1)

            def hw_lows(batch):
                for c in range(2):
                    dve.wait_ge(hw_high, batch * 2 + c + 1)
                    cols = slice(c * 512, (c + 1) * 512)
                    low(hwT_l[:, batch, cols], turn[:, c, :], hwT_h[:, batch, cols]).then_inc(hw_low, 1)

            dve.wait_ge(const_ready, 2)
            for name in start_vector_order(START):
                kind, n = name[0], pos.get(name)
                if name == ("V", 0, 0):
                    for c in range(KC):
                        dve.wait_ge(w_high, c + 1)
                        low(w_l[:, c, :], raw[:, c, :], w_h[:, c, :]).then_inc(w_low, 1)
                if kind == "bias":
                    dve.wait_ge(ring_filled, n + 1)
                    nc.vector.tensor_copy(bias[:], ring[:, n % 2, 0:NH + NKV]).then_inc(ring_emptied, 1)
                    dve.wait_ge(ring_emptied, n + 1)
                elif kind in ("K", "V"):
                    keys_or_values(name)
                elif kind == "stats":
                    ln_stats("x", name[1])
                elif kind == "norm":
                    ln_tile("x", name[1])
                else:
                    tile_low(name)
            dve.wait_ge(bc_loaded, 32)
            unit(0, 0, True)
            for T in range(1, UNITS):
                unit(0, T, False)
            with dve.Fori(1, NKV - 1) as g:
                for T in range(UNITS):
                    unit(g, T, False)
            for T in range(UNITS):
                unit(NKV - 1, T, False)
            for name in VECTOR_TAIL:
                kind, n = name[0], pos.get(name)
                if kind == "W":
                    add_to_y(n, n % 2, (UNITS - 1) * UT + name[1])
                elif kind == "e":
                    add_to_y(n, n % 2, name[1])
                elif kind == "stats":
                    ln_stats("f", name[1])
                elif kind == "norm":
                    ln_tile("f", name[1])
                elif kind == "f":
                    tile_low(name)
                elif kind == "A":
                    dve.wait_ge(small_high, 1)
                    low(fw_l[:, :, 0:ER], ring[:, n % 2, :].rearrange("p (c n) -> p c n", c=KC),
                        fw_h[:, :, 0:ER]).then_inc(ring_emptied, 1)
                elif kind == "router":
                    dve.wait_ge(small_high, 2)
                    low(fw_l[:, :, ER:FN], ring[:, n % 2, 0:KC * E].rearrange("p (c n) -> p c n", c=KC),
                        fw_h[:, :, ER:FN]).then_inc(ring_emptied, 1)
                elif kind == "Bm":
                    dve.wait_ge(small_high, 3)
                    low(bm_l, ring[:, n % 2, :], bm_h).then_inc(ring_emptied, 1)
                elif kind == "attend":
                    probs_low(NU)
                elif kind == "outputs":
                    outputs_low(NU)
                elif kind == "choice":
                    router_choice(name[1])
                elif kind == "gates":
                    router_gates(name[1])
                else:
                    hw_lows(name[1])

        @block.tensor
        def _(pe):
            mm = nc.tensor.matmul

            def passes(dst, stat, mov, start, stop):
                mm(dst, stat[0], mov[0], start=start, stop=False)
                mm(dst, stat[0], mov[1], start=False, stop=False)
                return mm(dst, stat[1], mov[0], start=False, stop=stop)

            def wait_slot(n):
                if not isinstance(n, int) or n >= 2:
                    pe.wait_ge(ring_emptied, n - 1)

            def turn_columns(dst, src, width=P):
                rows = src.shape[0]
                for c in range(KC):
                    last = nc.tensor.transpose(dst[:, c * width:(c + 1) * width], src[:, c * P:(c + 1) * P],
                                               ident[0:rows, 0:rows])
                return last

            def turn_tile(name):
                (kind, t), n = name, tile_no[name]
                if kind == "c":
                    pe.wait_ge(c_loaded[t % PTILES], 16 * (t // PTILES + 1))
                    src = c_stage[:, t % PTILES, :]
                else:
                    pe.wait_ge(xn_ready, norm_no[name] + 1)
                    src = xn[:, norm_no[name] % 2, :]
                if n >= 2:
                    pe.wait_ge(tile_emptied, n - 1)
                if kind == "f" and t < 2:
                    pe.wait_ge(p_low, NU * 2 - 1 + t)
                if kind == "f" and t >= TILES - 2:
                    pe.wait_ge(hw_low, t - (TILES - 2) + 1)
                turn_columns(turn[:, n % 2, :], src).then_inc(tile_filled, 1)

            def values(name):
                _, step, t = name
                n = pos[name]
                tile = ("c", step // CHUNKS * PTILES + t)
                pe.wait_ge(tile_emptied, tile_no[tile] + 1)
                wait_slot(n)
                tokens_h, tokens_l = turned_tile(tile)
                for c in range(KC):
                    if t == 0:
                        pe.wait_ge(w_low, step * KC + c + 1)
                    last = passes(ring[:, n % 2, :], (tokens_h[:, c], tokens_l[:, c]), (w_h[:, c, :], w_l[:, c, :]),
                                  c == 0, c == KC - 1)
                last.then_inc(ring_filled, 1)

            def keys(name):
                _, step, b, k = name
                n, cols = pos[name], slice(k * HD, (k + 1) * HD)
                wait_slot(n)
                for c in range(KC):
                    if b == 0 and k == 0:
                        pe.wait_ge(wo_low, step * KC + c + 1)
                    last = passes(ring[:, n % 2, :], (wo_h[:, c, cols], wo_l[:, c, cols]),
                                  (cT[b][0][:, c, :], cT[b][1][:, c, :]), c == 0, c == KC - 1)
                last.then_inc(ring_filled, 1)

            def queries(g, T, u, h):
                tok, cols = slice(T * UTOK, (T + 1) * UTOK), slice(h * HD, (h + 1) * HD)
                wait_slot(q_task(u, h))
                for c in range(KC):
                    if T == 0 and h == 0:
                        pe.wait_ge(w_low, (STEPS + g) * KC + c + 1)
                    last = passes(ring[:, q_slot(u, h), :], (w_h[:, c, cols], w_l[:, c, cols]),
                                  (xT_h[:, c, tok], xT_l[:, c, tok]), c == 0, c == KC - 1)
                last.then_inc(ring_filled, 1)

            def out_project(u, n, slot, i):
                pe.wait_ge(o_low, u * 4 - 3 + i)
                wait_slot(n)
                tok = slice(i * P, (i + 1) * P)
                for h in range(G):
                    last = passes(ring[:, slot, :], (oT_h[:, h, tok], oT_l[:, h, tok]),
                                  (wo_h[:, h, :], wo_l[:, h, :]), h == 0, h == G - 1)
                last.then_inc(ring_filled, 1)

            def scores(u, first):
                pe.wait_ge(ring_emptied, q_task(u, G - 1) + 1)
                pe.wait_ge(k_low, u + 1)
                if not first:
                    pe.wait_ge(o_low, u * 4)
                for b in range(UB):
                    for hp in range(HP):
                        dst = att_s[:, b * HP + hp]
                        q_h, q_l = (q[:, b, 2 * hp:2 * hp + 2, :].rearrange("p h l -> p (h l)") for q in (qT_h, qT_l))
                        mm(dst, q_h, kT[:, :, b, :], start=True, stop=False)
                        last = mm(dst, q_l, kT[:, :, b, :], start=False, stop=True)
                    if b % 2:
                        last.then_inc(scores_filled, 1)

            def turn_probs(u, first):
                for c in range(2):
                    pe.wait_ge(probs_ready, u * 2 + c + 1)
                    if not first:
                        pe.wait_ge(p_low, u * 2)
                    for b in range(4 * c, 4 * c + 4):
                        last = nc.tensor.transpose(turn[:, c, (b % 4) * P:(b % 4 + 1) * P],
                                                   s[:, HP * b:HP * b + HP, :].rearrange("p k l -> p (k l)"), ident[:])
                    last.then_inc(p_turned, 1)

            def outputs(u):
                pe.wait_ge(v_low, u)
                for b in range(UB):
                    if b % 4 == 0:
                        pe.wait_ge(p_low, u * 2 - 1 + b // 4)
                    dst = att[:, b // 2, (b % 2) * 256:(b % 2 + 1) * 256]
                    probs = pT[:, b, :, :].rearrange("p k l -> p (k l)")
                    mm(dst, v_h[:, b, :], probs, start=True, stop=False)
                    last = mm(dst, v_l[:, b, :], probs, start=False, stop=True)
                    if b % 2:
                        last.then_inc(o_filled, 1)

            def unit(g, T, first):
                u = g * UNITS + T
                second = isinstance(u, int) and u == 1
                queries(g, T, u, 0)
                if second:
                    turn_probs(0, True)
                    queries(g, T, u, 1)
                if not first:
                    outputs(u)
                if not second:
                    queries(g, T, u, 1)
                for h in range(2, G):
                    queries(g, T, u, h)
                if T == 1:
                    pe.wait_ge(wo_low, (STEPS + g) * KC + KC)
                if not first:
                    out_project(u, out_task(u, 0), out_slot(0), 0)
                scores(u, first)
                if not first:
                    for i in range(1, UT):
                        out_project(u, out_task(u, i), out_slot(i), i)
                if not first:
                    turn_probs(u, first)

            def down(t):
                bank, place = expert_place(t)
                if t < ETILES + 3:
                    pe.wait_ge(o_low, NU * 4)
                else:
                    pe.wait_ge(hw_ready, bank + 1)
                pe.wait_ge(ring_emptied, pos["Bm",] + 1)
                pe.wait_ge(tile_emptied, tile_no["f", t] + 1)
                sl = slice(t * P, (t + 1) * P)
                for c in range(KC):
                    last = passes(att_f[:, bank, place, :], (xT_h[:, c, sl], xT_l[:, c, sl]),
                                  (fw_h[:, c, :], fw_l[:, c, :]), c == 0, c == KC - 1)
                last.then_inc(experts_filled, 1)

            def turn_products(batch):
                for c in range(2):
                    pe.wait_ge(hw_ready, batch * 3 + 2 + c)
                    pe.wait_ge(tile_emptied, tile_no["f", TILES - 3 if batch == 0 else TILES - 1] + 1)
                    for t in range(4 * c, 4 * c + 4):
                        last = nc.tensor.transpose(turn[:, c, (t % 4) * P:(t % 4 + 1) * P], hw[:, t, :], ident[:])
                    last.then_inc(hw_turned, 1)

            def up(t):
                n, batch, i = pos["e", t], t // ETILES, t % ETILES
                pe.wait_ge(hw_low, batch * 2 + i // 4 + 1)
                wait_slot(n)
                sl = slice(i * P, (i + 1) * P)
                passes(ring[:, n % 2, :], (hwT_h[:, batch, sl], hwT_l[:, batch, sl]), (bm_h, bm_l),
                       True, True).then_inc(ring_filled, 1)

            pe.wait_ge(ident_ready, 1)
            for name in START:
                kind, n = name[0], pos.get(name)
                if kind == "bias":
                    rows = NH + NKV
                    wait_slot(n)
                    pe.wait_ge(bias_loaded, 48)
                    nc.tensor.transpose(ring[:, n % 2, 0:rows], bias_rows, ident[0:rows, 0:rows]).then_inc(ring_filled, 1)
                elif kind == "V":
                    values(name)
                elif kind == "K":
                    keys(name)
                else:
                    turn_tile(name)
            pe.wait_ge(tile_emptied, tile_no["x", TILES - 1] + 1)
            unit(0, 0, True)
            for T in range(1, UNITS):
                unit(0, T, False)
            with pe.Fori(1, NKV - 1) as g:
                for T in range(UNITS):
                    unit(g, T, False)
            for T in range(UNITS):
                unit(NKV - 1, T, False)
            for name in TENSOR_TAIL:
                kind, n = name[0], pos.get(name)
                if kind == "attend":
                    outputs(NU)
                elif kind == "W":
                    out_project(NU, n, n % 2, name[1])
                elif kind == "A":
                    pe.wait_ge(small_loaded, 16 * (2 + KC))
                    wait_slot(n)
                    turn_columns(ring[:, n % 2, :], a_rows).then_inc(ring_filled, 1)
                elif kind == "router":
                    wait_slot(n)
                    turn_columns(ring[:, n % 2, :], router_rows, E).then_inc(ring_filled, 1)
                elif kind == "Bm":
                    wait_slot(n)
                    turn_columns(ring[:, n % 2, :], bm_rows).then_inc(ring_filled, 1)
                elif kind == "f":
                    turn_tile(name)
                elif kind == "down":
                    down(name[1])
                elif kind == "products":
                    turn_products(name[1])
                else:
                    up(name[1])


_INS = ["x", "ctx_4096", "L0_xattn_Wq", "L0_xattn_bq", "L0_xattn_Wkv", "L0_xattn_bkv", "L0_xattn_Wo", "L0_xattn_bo",
        "L0_ffn_router_w", "L0_ffn_router_b", "L0_ffn_A", "L0_ffn_Bm"]


def kernel(**inputs):
    import numpy as _np
    import concourse.bacc as _bacc
    from concourse import mybir as _mybir
    from concourse.bass_utils import run_bass_kernel_spmd as _run

    nc = _bacc.Bacc("TRN2", target_bir_lowering=False, num_devices=1)
    arrays, args = {}, []
    for name in _INS:
        a = _np.ascontiguousarray(inputs[name])
        arrays[f"in_{name}_dram"] = a
        args.append(nc.dram_tensor(f"in_{name}_dram", a.shape, _mybir.dt.from_np(a.dtype), kind="ExternalInput").ap())
    args.append(nc.dram_tensor("out_dram", (B, L, D), F32, kind="ExternalOutput").ap())
    args.append(nc.dram_tensor("keys_dram", (NKV * HD, TOK), F32, kind="Internal").ap())
    args.append(nc.dram_tensor("values_dram", (NKV * L, B * HD), F32, kind="Internal").ap())
    build(nc, *args)
    r = _run(nc, [arrays], core_ids=[0])
    return r.results[0]["out_dram"]
```
